# Optimizing a Trainium2 kernel written in Bass

```python
import numpy as np
import jax
import jax.numpy as jnp

def _softmax(x, axis=-1):
    return jax.nn.softmax(x, axis=axis)

def _gelu(x):
    return jax.nn.gelu(x, approximate=True)

def _silu(x):
    return jax.nn.silu(x)

def _sigmoid(x):
    return jax.nn.sigmoid(x)

def _layernorm(x, axis=-1, eps=1e-05):
    m = jnp.mean(x, axis=axis, keepdims=True)
    v = jnp.var(x, axis=axis, keepdims=True)
    return (x - m) / jnp.sqrt(v + eps)

def _scatter_add(tgt, idx, src, axis=0):
    return tgt.at[idx].add(src)

def _segment_sum(src, seg, n):
    return jax.ops.segment_sum(src, seg, n)
kernel_name = 'mk_xattn_ffn_d2_seqx_r8_d4ed20'

def setup_inputs(seed: int=0):
    np.random.seed(seed)
    _w = jnp.asarray

    def _rec_inputs():
        import jax
        import jax.numpy as jnp
        _rk = jax.random.key(seed)
        x = 7.22e-05 + 1 * jax.random.normal(jax.random.fold_in(_rk, 1), (2, 512, 128), jnp.float32)
        _lenS = 512 - jax.random.randint(jax.random.fold_in(_rk, 7), (2,), 0, max(1, 512 // 4) + 1, jnp.int32)
        _lenS2 = 32 - jax.random.randint(jax.random.fold_in(_rk, 8), (2,), 0, max(1, 32 // 4) + 1, jnp.int32)
        _ctx_768P = jax.random.normal(jax.random.fold_in(_rk, 11), (2, 16, 96), jnp.float32)
        _ctx_768c = jax.random.dirichlet(jax.random.fold_in(_rk, 511), 0.3 * jnp.ones((16,), jnp.float32), (2, 32))
        _ctx_768t = jnp.einsum('bsk,bkd->bsd', _ctx_768c, _ctx_768P)
        _ctx_768t = _ctx_768t * jax.lax.rsqrt(jnp.mean(jnp.square(_ctx_768t)) + 1e-12) * 0.953939
        ctx_768 = -0.000191848 + 0.999787 * (_ctx_768t + 0.3 * jax.random.normal(jax.random.fold_in(_rk, 611), (2, 32, 96), jnp.float32))
        return (x, ctx_768)
    x, ctx_768 = _rec_inputs()

    def _L0_xattn_setup():
        import jax, jax.numpy as jnp
        import numpy as np
        B, LQ, LK = (4, 256, 256)
        D1, D2, H = (128, 96, 128)
        key = jax.random.key(seed)
        ks = jax.random.split(key, 9)
        s1, s2, sh = (1.0 / np.sqrt(D1), 1.0 / np.sqrt(D2), 1.0 / np.sqrt(H))
        return {'query': jax.random.normal(ks[0], (B, LQ, D1), jnp.float32), 'key': jax.random.normal(ks[1], (B, LK, D2), jnp.float32), 'value': jax.random.normal(ks[2], (B, LK, D2), jnp.float32), 'Wq': jax.random.normal(ks[3], (D1, H), jnp.float32) * s1, 'bq': jax.random.normal(ks[4], (H,), jnp.float32) * s1, 'Wk': jax.random.normal(ks[5], (D2, H), jnp.float32) * s2, 'bk': jax.random.normal(ks[6], (H,), jnp.float32) * s2, 'Wv': jax.random.normal(ks[7], (D2, H), jnp.float32) * s2, 'bv': jax.random.normal(ks[8], (H,), jnp.float32) * s2}
    _L0_xattn_all = _L0_xattn_setup()
    _L0_xattn_in = {k: v for k, v in _L0_xattn_all.items() if k in ('Wq', 'bq', 'Wk', 'bk', 'Wv', 'bv')}
    del _L0_xattn_all

    def _L0_ffn_setup():
        import jax, jax.numpy as jnp
        import numpy as np
        from jax import lax
        T, B, I, M, O = (32, 64, 128, 128, 128)

        def _xavier(key, shape):
            fan_out, fan_in = shape
            limit = float(np.sqrt(6.0 / (fan_in + fan_out)))
            return jax.random.uniform(key, shape, jnp.float32, -limit, limit)
        key = jax.random.key(seed)
        ks = jax.random.split(key, 9)
        x = jax.random.normal(ks[0], (T, B, I), jnp.float32)
        return {'x': x, 'wf': _xavier(ks[1], (M, I)), 'uf': _xavier(ks[2], (M, M)), 'bf': jnp.zeros((M,), jnp.float32), 'wi': _xavier(ks[3], (M, I)), 'ui': _xavier(ks[4], (M, M)), 'bi': jnp.zeros((M,), jnp.float32), 'wc': _xavier(ks[5], (M, I)), 'uc': _xavier(ks[6], (M, M)), 'bc': jnp.zeros((M,), jnp.float32), 'wo': _xavier(ks[7], (O, I)), 'uo': _xavier(ks[8], (O, M)), 'bo': jnp.zeros((O,), jnp.float32), 'in_c': jnp.zeros((M,), jnp.float32)}
    _L0_ffn_all = _L0_ffn_setup()
    _L0_ffn_in = {k: v for k, v in _L0_ffn_all.items() if k in ('wf', 'uf', 'bf', 'wi', 'ui', 'bi', 'wc', 'uc', 'bc', 'wo', 'uo', 'bo', 'in_c')}
    del _L0_ffn_all

    def _L1_xattn_setup():
        import jax, jax.numpy as jnp
        import numpy as np
        HEADS = 16
        DIM_HEAD = 64
        QUERY_DIM = 128
        CONTEXT_DIM = 96
        INNER = HEADS * DIM_HEAD
        SCALE = DIM_HEAD ** (-0.5)
        key = jax.random.key(seed)
        ks = jax.random.split(key, 7)
        B, Sq, Skv = (4, 256, 256)
        x = jax.random.normal(ks[0], (B, Sq, QUERY_DIM), dtype=jnp.float32)
        context = jax.random.normal(ks[1], (B, Skv, CONTEXT_DIM), dtype=jnp.float32)
        w_q = jax.random.normal(ks[2], (QUERY_DIM, INNER), dtype=jnp.float32) / np.sqrt(QUERY_DIM)
        w_k = jax.random.normal(ks[3], (CONTEXT_DIM, INNER), dtype=jnp.float32) / np.sqrt(CONTEXT_DIM)
        w_v = jax.random.normal(ks[4], (CONTEXT_DIM, INNER), dtype=jnp.float32) / np.sqrt(CONTEXT_DIM)
        w_o = jax.random.normal(ks[5], (INNER, QUERY_DIM), dtype=jnp.float32) / np.sqrt(INNER)
        b_o = jax.random.normal(ks[6], (QUERY_DIM,), dtype=jnp.float32) * 0.02
        return {'x': x, 'context': context, 'w_q': w_q, 'w_k': w_k, 'w_v': w_v, 'w_o': w_o, 'b_o': b_o}
    _L1_xattn_all = _L1_xattn_setup()
    _L1_xattn_in = {k: v for k, v in _L1_xattn_all.items() if k in ('w_q', 'w_k', 'w_v', 'w_o', 'b_o')}
    del _L1_xattn_all

    def _L1_ffn_setup():
        import jax, jax.numpy as jnp
        import numpy as np
        D_MODEL = 128
        N_EXPERTS = 8
        TOP_K = 2
        FFN_HIDDEN = 4 * D_MODEL
        key = jax.random.key(seed)
        ks = jax.random.split(key, 6)

        def xavier(k, shape):
            fan_in, fan_out = (shape[-2], shape[-1])
            lim = jnp.sqrt(6.0 / (fan_in + fan_out))
            return jax.random.uniform(k, shape, jnp.float32, -lim, lim)
        x = jax.random.normal(ks[0], (4, 256, D_MODEL), jnp.float32)
        w_gate = xavier(ks[1], (N_EXPERTS, D_MODEL))
        W1 = xavier(ks[2], (N_EXPERTS, D_MODEL, FFN_HIDDEN))
        b1 = jnp.zeros((N_EXPERTS, FFN_HIDDEN), jnp.float32)
        W2 = xavier(ks[3], (N_EXPERTS, FFN_HIDDEN, D_MODEL))
        b2 = jnp.zeros((N_EXPERTS, D_MODEL), jnp.float32)
        return {'x': x, 'w_gate': w_gate, 'W1': W1, 'b1': b1, 'W2': W2, 'b2': b2}
    _L1_ffn_all = _L1_ffn_setup()
    _L1_ffn_in = {k: v for k, v in _L1_ffn_all.items() if k in ('w_gate', 'W1', 'b1', 'W2', 'b2')}
    del _L1_ffn_all
    return {'x': x, 'ctx_768': ctx_768, 'L0_xattn_Wq': _L0_xattn_in['Wq'], 'L0_xattn_bq': _L0_xattn_in['bq'], 'L0_xattn_Wk': _L0_xattn_in['Wk'], 'L0_xattn_bk': _L0_xattn_in['bk'], 'L0_xattn_Wv': _L0_xattn_in['Wv'], 'L0_xattn_bv': _L0_xattn_in['bv'], 'L0_ffn_wf': _L0_ffn_in['wf'], 'L0_ffn_uf': _L0_ffn_in['uf'], 'L0_ffn_bf': _L0_ffn_in['bf'], 'L0_ffn_wi': _L0_ffn_in['wi'], 'L0_ffn_ui': _L0_ffn_in['ui'], 'L0_ffn_bi': _L0_ffn_in['bi'], 'L0_ffn_wc': _L0_ffn_in['wc'], 'L0_ffn_uc': _L0_ffn_in['uc'], 'L0_ffn_bc': _L0_ffn_in['bc'], 'L0_ffn_wo': _L0_ffn_in['wo'], 'L0_ffn_uo': _L0_ffn_in['uo'], 'L0_ffn_bo': _L0_ffn_in['bo'], 'L0_ffn_in_c': _L0_ffn_in['in_c'], 'L1_xattn_w_q': _L1_xattn_in['w_q'], 'L1_xattn_w_k': _L1_xattn_in['w_k'], 'L1_xattn_w_v': _L1_xattn_in['w_v'], 'L1_xattn_w_o': _L1_xattn_in['w_o'], 'L1_xattn_b_o': _L1_xattn_in['b_o'], 'L1_ffn_w_gate': _L1_ffn_in['w_gate'], 'L1_ffn_W1': _L1_ffn_in['W1'], 'L1_ffn_b1': _L1_ffn_in['b1'], 'L1_ffn_W2': _L1_ffn_in['W2'], 'L1_ffn_b2': _L1_ffn_in['b2']}

def reference(x, ctx_768, L0_xattn_Wq, L0_xattn_bq, L0_xattn_Wk, L0_xattn_bk, L0_xattn_Wv, L0_xattn_bv, L0_ffn_wf, L0_ffn_uf, L0_ffn_bf, L0_ffn_wi, L0_ffn_ui, L0_ffn_bi, L0_ffn_wc, L0_ffn_uc, L0_ffn_bc, L0_ffn_wo, L0_ffn_uo, L0_ffn_bo, L0_ffn_in_c, L1_xattn_w_q, L1_xattn_w_k, L1_xattn_w_v, L1_xattn_w_o, L1_xattn_b_o, L1_ffn_w_gate, L1_ffn_W1, L1_ffn_b1, L1_ffn_W2, L1_ffn_b2):
    import jax
    import jax.numpy as jnp

    def _L0_xattn_ref(query, key, value, Wq, bq, Wk, bk, Wv, bv):
        import jax, jax.numpy as jnp
        import numpy as np
        B, LQ, LK = (4, 256, 256)
        D1, D2, H = (128, 96, 128)
        q = jnp.einsum('bqd,dh->bqh', query, Wq) + bq
        k = jnp.einsum('bkd,dh->bkh', key, Wk) + bk
        v = jnp.einsum('bkd,dh->bkh', value, Wv) + bv
        scores = jnp.einsum('bqh,bkh->bqk', q, k)
        weights = jax.nn.softmax(scores, axis=-1)
        return jnp.einsum('bqk,bkh->bqh', weights, v)

    def _L0_ffn_ref(x, wf, uf, bf, wi, ui, bi, wc, uc, bc, wo, uo, bo, in_c):
        import jax, jax.numpy as jnp
        import numpy as np
        from jax import lax
        T, B, I, M, O = (32, 64, 128, 128, 128)

        def _xavier(key, shape):
            fan_out, fan_in = shape
            limit = float(np.sqrt(6.0 / (fan_in + fan_out)))
            return jax.random.uniform(key, shape, jnp.float32, -limit, limit)
        batch = x.shape[1]
        c0 = jnp.broadcast_to(in_c, (batch, in_c.shape[0]))

        def step(c, xt):
            ft = jax.nn.sigmoid(xt @ wf.T + c @ uf.T + bf)
            it = jax.nn.sigmoid(xt @ wi.T + c @ ui.T + bi)
            gt = jnp.tanh(xt @ wc.T + c @ uc.T + bc)
            c = ft * c + it * gt
            return (c, None)
        c_final, _ = lax.scan(step, c0, x)
        h = jnp.tanh(jnp.einsum('tbi,oi->tbo', x, wo) + c_final @ uo.T + bo)
        return h

    def _L1_xattn_ref(x, context, w_q, w_k, w_v, w_o, b_o):
        import jax, jax.numpy as jnp
        import numpy as np
        HEADS = 16
        DIM_HEAD = 64
        QUERY_DIM = 128
        CONTEXT_DIM = 96
        INNER = HEADS * DIM_HEAD
        SCALE = DIM_HEAD ** (-0.5)
        B, Sq, _ = x.shape
        Skv = context.shape[1]
        q = (x @ w_q).reshape(B, Sq, HEADS, DIM_HEAD).transpose(0, 2, 1, 3)
        k = (context @ w_k).reshape(B, Skv, HEADS, DIM_HEAD).transpose(0, 2, 1, 3)
        v = (context @ w_v).reshape(B, Skv, HEADS, DIM_HEAD).transpose(0, 2, 1, 3)
        sim = jnp.einsum('bhid,bhjd->bhij', q, k) * SCALE
        attn = jax.nn.softmax(sim, axis=-1)
        out = jnp.einsum('bhij,bhjd->bhid', attn, v)
        out = out.transpose(0, 2, 1, 3).reshape(B, Sq, INNER)
        return out @ w_o + b_o

    def _L1_ffn_ref(x, w_gate, W1, b1, W2, b2):
        import jax, jax.numpy as jnp
        import numpy as np
        D_MODEL = 128
        N_EXPERTS = 8
        TOP_K = 2
        FFN_HIDDEN = 4 * D_MODEL
        B, S, D = x.shape
        flat_x = x.reshape(-1, D)
        gate = jax.nn.softmax(flat_x @ w_gate.T, axis=-1)
        topk_scores, topk_idx = jax.lax.top_k(gate, TOP_K)
        cw = (jax.nn.one_hot(topk_idx, N_EXPERTS, dtype=flat_x.dtype) * topk_scores[..., None]).sum(axis=1)
        h = jax.nn.gelu(jnp.einsum('td,edh->teh', flat_x, W1) + b1, approximate=False)
        y = jnp.einsum('teh,ehd->ted', h, W2) + b2
        out = jnp.einsum('ted,te->td', y, cw)
        return out.reshape(B, S, D)
    x = x + _L0_xattn_ref(_layernorm(x, axis=-1), ctx_768, ctx_768, L0_xattn_Wq, L0_xattn_bq, L0_xattn_Wk, L0_xattn_bk, L0_xattn_Wv, L0_xattn_bv)
    x = x + _L0_ffn_ref(_layernorm(x, axis=-1), L0_ffn_wf, L0_ffn_uf, L0_ffn_bf, L0_ffn_wi, L0_ffn_ui, L0_ffn_bi, L0_ffn_wc, L0_ffn_uc, L0_ffn_bc, L0_ffn_wo, L0_ffn_uo, L0_ffn_bo, L0_ffn_in_c)
    x = x + _L1_xattn_ref(_layernorm(x, axis=-1), ctx_768, L1_xattn_w_q, L1_xattn_w_k, L1_xattn_w_v, L1_xattn_w_o, L1_xattn_b_o)
    x = x + _L1_ffn_ref(_layernorm(x, axis=-1), L1_ffn_w_gate, L1_ffn_W1, L1_ffn_b1, L1_ffn_W2, L1_ffn_b2)
    return x

_drawn_inputs = setup_inputs


def setup_inputs(seed=0):
    import zlib

    import numpy as np

    out = dict(_drawn_inputs(seed))
    spreads = {'L0_ffn_bf': (0.0, 0.8),
     'L0_ffn_bi': (0.0, 0.758),
     'L0_ffn_bc': (0.0, 0.434),
     'L0_ffn_bo': (0.0, 0.1),
     'L0_ffn_in_c': (0.0, 0.428),
     'L1_ffn_b1': (0.0, 0.32),
     'L1_ffn_b2': (0.0, 0.1)}
    factors = {'L0_xattn_bk': 8.0, 'L0_ffn_uf': 4.889, 'L0_ffn_ui': 3.04, 'L1_xattn_b_o': 3.823}
    for name, (base, spread) in spreads.items():
        noise = np.random.default_rng([zlib.crc32(name.encode()), seed]).standard_normal(out[name].shape)
        drawn = base * np.exp(spread * noise) if base else spread * noise
        out[name] = jnp.asarray(drawn.astype(out[name].dtype))
    for name, factor in factors.items():
        out[name] = (out[name] * factor).astype(out[name].dtype)
    return out
```

```python
from contextlib import ExitStack

import concourse.bass as bass
from concourse import mybir

F32 = mybir.dt.float32
F32R = mybir.dt.float32r
ALU = mybir.AluOpType
ACT = mybir.ActivationFunctionType
X = mybir.AxisListType.X

P = 128
B = 2
S = 512
T = S // P
D = 128
C = 96
J = 32
H = 16
DH = 64
HC = H * DH // P
KC = H * J // P
HPC = P // J
E = 8
F = 512
FC = F // P
STEPS = E * FC
LAG = 2
PAIR = 2 * FC
EPS = 1e-5


def two_layers(nc, i, out):
    ctx = ExitStack()
    with ctx:
        def sb(name, shape, dt=F32):
            return ctx.enter_context(nc.sbuf_tensor(name, shape, dt))

        def sem(name):
            return ctx.enter_context(nc.semaphore(name))

        psum = ctx.enter_context(nc.psum_tensor("psum", [P, 8, 512], F32))

        def bank(n):
            return psum[:, n, :]

        x = sb("x", [P, B, T, D])
        xn = sb("xn", [P, B, T, D])
        xnT = sb("xnT", [D, B, S])
        stats = sb("stats", [P, B, T, 6])
        moments = sb("moments", [P, B, T, 2])
        var_eps = sb("var_eps", [P, B, T])
        minus_half = sb("minus_half", [P, T])
        rstd = sb("rstd", [P, B, T])
        ident = sb("ident", [P, P])

        def overlay(name, shapes, whole):
            words = whole[1]
            for d in whole[2:]:
                words *= d
            space, at, views = sb(name, [P, words]), 0, []
            for shape in [whole, *shapes]:
                n = 1
                for d in shape[1:]:
                    n *= d
                start = 0 if shape is whole else at
                at = at if shape is whole else at + n
                assert at <= words
                names = " ".join("abcd"[:len(shape) - 1])
                sizes = dict(zip("bcd", shape[2:]))
                views.append(space[0:shape[0], start:start + n].rearrange(f"p ({names}) -> p {names}", **sizes))
            return views
        ones = sb("ones", [P, P])
        bandmask = sb("bandmask", [P, T])

        ctx_rows = sb("ctx_rows", [B * J, C])
        ctxT = sb("ctxT", [C + 1, B, T, J])
        wq0 = sb("wq0", [D, D])
        wq0T = sb("wq0T", [D, D])
        wk0 = sb("wk0", [C + 1, D])
        wv0 = sb("wv0", [C + 1, D])
        bq0 = sb("bq0", [D, 1])
        bq0_wide = sb("bq0_wide", [D, P])
        k0T = sb("k0T", [D, B, J])
        v0_band = sb("v0_band", [P, B, T, D])
        key0 = sb("key0", [D, B, J])

        gate_w = sb("gate_w", [D, 8, D])
        gate_wT = sb("gate_wT", [D, 4, D])
        gate_uT = sb("gate_uT", [D, 4, D])
        bias_f = sb("bias_f", [D, 4])
        in_c = sb("in_c", [D, 1])
        c0x2 = sb("c0x2", [D, 1])
        bias_t0 = sb("bias_t0", [D, 3])
        bias_t1 = sb("bias_t1", [D, 3])

        bo1 = sb("bo1", [P, D])
        wq1T = sb("wq1T", [P, HC, D])
        k1_band = sb("k1_band", [P, HC, 2, B * J])
        key1 = sb("key1", [D, B, H, J])
        val1 = sb("val1", [P, B, KC, D])

        shifted0 = sb("shifted0", [P, B, T, J])
        probs0 = sb("probs0", [P, B, T, J])
        probs0T = sb("probs0T", [P, B, P])
        small0 = sb("small0", [P, 3, B, T])
        shifted1 = sb("shifted1", [P, 2, H, J])
        probs1 = sb("probs1", [P, 2, H, J])
        probs1T = sb("probs1T", [P, 2, KC, P])
        small1 = sb("small1", [P, 3, 2, H])

        wg = sb("wg", [E, D])
        wgT = sb("wgT", [D, 2, E], F32R)
        xh = sb("xh", [D, B * S], F32R)
        xl = sb("xl", [D, B * S], F32R)
        g_shift = sb("g_shift", [P, B, T, E])
        g_prob = sb("g_prob", [P, B, T, E])
        g_small = sb("g_small", [P, 4, B, T])
        g_eq = sb("g_eq", [P, B, T, E])
        g_first = sb("g_first", [P, B, T, E])
        g_rest = sb("g_rest", [P, B, T, E])
        descend = sb("descend", [P, E])
        combine = sb("combine", [P, B, T, E])
        combineT = sb("combineT", [E, B * S])
        cwb, gates, keep_c, new_c, c1x2, c2x2, hT, v1_band = overlay("cwb", [
            [D, 2, 3, S], [D, S], [D, S], [D, S], [D, S], [D, B, S], [P, HC, B, HPC, J]], [P, E, B * S])
        hid, wk1, wv1 = overlay("hid", [[C, HC, P], [C, HC, P]], [P, 2, B * S])
        part, wo1 = overlay("part", [[P, HC, D]], [P, 2, S])
        acc, wq1 = overlay("acc", [[D, HC, P]], [D, B * S])
        combine_dram = nc.dram_tensor("combine_dram", [E, B * S], F32, kind="Internal").ap()

        w1 = sb("w1", [D, E, F])
        w2 = sb("w2", [P, E, FC, D])
        b1 = sb("b1", [P, E, FC])
        b2 = sb("b2", [E, D])
        w1h = sb("w1h", [D, 2, FC, P], F32R)
        w1l = sb("w1l", [D, 2, FC, P], F32R)
        w2h = sb("w2h", [P, 2, FC, D], F32R)
        w2l = sb("w2l", [P, 2, FC, D], F32R)
        hh = sb("hh", [P, 4, B * S], F32R)
        hl = sb("hl", [P, 4, B * S], F32R)

        x_in = [sem(f"x_in{b}") for b in range(B)]
        ctx_in, wq0_in, kv0_in, ffn_in, ffb_in = sem("ctx_in"), sem("wq0_in"), sem("kv0_in"), sem("ffn_in"), sem("ffb_in")
        wq1_in, wkv1_in, wo1_in, bo1_in = sem("wq1_in"), sem("wkv1_in"), sem("wo1_in"), sem("bo1_in")
        gate_in, w1_in, w2_in = sem("gate_in"), [sem(f"w1_in{n}") for n in range(2)], [sem(f"w2_in{n}") for n in range(2)]
        b1_in, b2_in = sem("b1_in"), sem("b2_in")
        cwb_in, combine_out, out_done = [sem(f"cwb_in{n}") for n in range(2)], sem("combine_out"), sem("out_done")
        const_ready, pool_step = sem("const_ready"), sem("pool_step")
        dve_step = sem("dve_step")
        turn_psum, ctxT_ready, gate_wT_ready = sem("turn_psum"), sem("ctxT_ready"), sem("gate_wT_ready")
        const_psum, bias_ready, bq_wide_ready = sem("const_psum"), sem("bias_ready"), sem("bq_wide_ready")
        kv0_psum, k0_ready, v0_ready = sem("kv0_psum"), sem("k0_ready"), sem("v0_ready")
        key0_psum, key0_ready = sem("key0_psum"), sem("key0_ready")
        wq1T_psum, wq1T_ready = sem("wq1T_psum"), sem("wq1T_ready")
        band_zero, c0x2_ready = sem("band_zero"), sem("c0x2_ready")
        kv1_psum, k1_ready, v1_ready = sem("kv1_psum"), sem("k1_ready"), sem("v1_ready")
        key1_psum, key1_ready = sem("key1_psum"), sem("key1_ready")
        val1_psum, val1_ready = sem("val1_psum"), sem("val1_ready")
        moments_ready, rstd_ready, xn_ready = sem("moments_ready"), sem("rstd_ready"), sem("xn_ready")
        xnT_psum, xnT_ready = sem("xnT_psum"), sem("xnT_ready")
        s0_psum, sh0_ready, e0_ready, p0_ready = sem("s0_psum"), sem("sh0_ready"), sem("e0_ready"), sem("p0_ready")
        p0T_psum, p0T_ready, o0_psum = sem("p0T_psum"), sem("p0T_ready"), sem("o0_psum")
        z_psum, gates_ready, c_ready = sem("z_psum"), sem("gates_ready"), sem("c_ready")
        ho_psum, hT_ready, h_psum = sem("ho_psum"), sem("hT_ready"), sem("h_psum")
        x2_ready, x2b_ready = sem("x2_ready"), sem("x2b_ready")
        s1_psum, sh1_ready, e1_ready, r1_ready, p1_ready = (sem("s1_psum"), sem("sh1_ready"), sem("e1_ready"),
                                                            sem("r1_ready"), sem("p1_ready"))
        p1T_psum, p1T_ready, o1_step = sem("p1T_psum"), sem("p1T_ready"), sem("o1_step")
        xl_ready = sem("xl_ready")
        logit_psum, gexp_arg, gexp_ready = sem("logit_psum"), sem("gexp_arg"), sem("gexp_ready")
        combine_ready, combineT_psum, combineT_ready = sem("combine_ready"), sem("combineT_psum"), sem("combineT_ready")
        b2_psum, acc_ready = sem("b2_psum"), sem("acc_ready")
        w1_split, w2_split = sem("w1_split"), sem("w2_split")
        mm1_done, mm2_done = sem("mm1_done"), sem("mm2_done")
        gelu_done, hi_done, lo_done = sem("gelu_done"), sem("hi_done"), sem("lo_done")
        y_used, sum_ready, y_turned, res_ready = sem("y_used"), sem("sum_ready"), sem("y_turned"), sem("res_ready")

        x_v = i["x"].rearrange("b (p i) d -> b p i d", i=T)
        out_v = out.rearrange("b (p i) d -> b p i d", i=T)
        w2_v = i["L1_ffn_W2"].rearrange("e (p c) d -> p e c d", c=FC)
        b1_v = i["L1_ffn_b1"].rearrange("e (p c) -> p e c", c=FC)
        w1_v = i["L1_ffn_W1"].rearrange("e d f -> d e f")

        def column(a):
            return a.rearrange("(d a) -> d a", a=1)

        block = ctx.enter_context(nc.Block())

        @block.sync
        def _(sp):
            sp.dma_start(ctx_rows[:, :], i["ctx_768"].rearrange("b j c -> (b j) c")).then_inc(ctx_in, 16)
            sp.dma_start(x[:, 0], x_v[0]).then_inc(x_in[0], 16)
            sp.dma_start(x[:, 1], x_v[1]).then_inc(x_in[1], 16)
            sp.dma_start(wk0[0:C, :], i["L0_xattn_Wk"]).then_inc(kv0_in, 16)
            sp.dma_start(wk0[C:C + 1, :], i["L0_xattn_bk"].rearrange("(a d) -> a d", a=1)).then_inc(kv0_in, 16)
            for n, name in enumerate(("wf", "wi", "wc", "wo", "uf", "ui", "uc", "uo")):
                sp.dma_start(gate_w[:, n, :], i["L0_ffn_" + name]).then_inc(ffn_in, 16)
            sp.dma_start(wq1[:, :, :], i["L1_xattn_w_q"].rearrange("d (c n) -> d c n", c=HC)).then_inc(wq1_in, 16)
            sp.dma_start(wk1[:, :, :], i["L1_xattn_w_k"].rearrange("d (c n) -> d c n", c=HC)).then_inc(wkv1_in, 16)
            sp.dma_start(wv1[:, :, :], i["L1_xattn_w_v"].rearrange("d (c n) -> d c n", c=HC)).then_inc(wkv1_in, 16)
            sp.dma_start(wo1[:, :, :], i["L1_xattn_w_o"].rearrange("(c p) d -> p c d", c=HC)).then_inc(wo1_in, 16)
            sp.dma_start(bo1[:, :], i["L1_xattn_b_o"].partition_broadcast(P)).then_inc(bo1_in, 16)
            for n, es in enumerate((slice(0, 2), slice(2, E))):
                sp.dma_start(w1[:, es], w1_v[:, es]).then_inc(w1_in[n], 16)
                sp.dma_start(w2[:, es], w2_v[:, es]).then_inc(w2_in[n], 16)
            sp.wait_ge(combineT_ready, B)
            sp.dma_start(combine_dram, combineT[:, :]).then_inc(combine_out, 16)
            sp.wait_ge(combine_out, 16)
            for n, (e, m) in enumerate(((0, 2), (2, E - 2))):
                sp.dma_start(cwb[:, e:e + m, :], combine_dram[e:e + m, :].partition_broadcast(P)).then_inc(cwb_in[n], 16)
            for b in range(B):
                sp.wait_ge(res_ready, b + 1)
                sp.dma_start(out_v[b], x[:, b]).then_inc(out_done, 16)
            sp.wait_ge(out_done, 16 * B)

        @block.gpsimd
        def _(pool):
            steps = [0]

            def done(ins):
                steps[0] += 1
                ins.then_inc(pool_step, 1)
                pool.wait_ge(pool_step, steps[0])

            done(pool.memset(ones[:, :], 1.0))
            pool.affine_select(out=ident[:, :], in_=ones[:, :], compare_op=ALU.is_equal, fill=0.0, base=0,
                               pattern=[[-1, P]], channel_multiplier=1).then_inc(const_ready, 1)
            pool.wait_ge(const_ready, 1)
            pool.memset(ctxT[C:C + 1, :, :, :], 1.0).then_inc(const_ready, 1)
            pool.wait_ge(const_ready, 2)
            pool.memset(minus_half[:, :], -0.5)
            done(pool.affine_select(out=bandmask[:, :], in_=ones[:, 0:T], compare_op=ALU.is_ge, fill=0.0, base=0,
                                    pattern=[[-J, T]], channel_multiplier=1))
            pool.affine_select(out=bandmask[:, :], in_=bandmask[:, :], compare_op=ALU.is_ge, fill=0.0, base=J - 1,
                               pattern=[[J, T]], channel_multiplier=-1).then_inc(const_ready, 1)
            pool.iota(descend[:, :], pattern=[[-1, E]], base=E, channel_multiplier=0,
                      allow_small_or_imprecise_dtypes=True).then_inc(const_ready, 1)
            pool.wait_ge(wq0_in, 32)
            pool.tensor_scalar(bq0_wide[:, :], ones[:, :], bq0[:, 0:1], None, ALU.mult).then_inc(bq_wide_ready, 1)
            pool.memset(k1_band[:, :, :, :], 0.0)
            pool.memset(v1_band[:, :, :, :, :], 0.0).then_inc(band_zero, 1)

            def split(w, hi, lo, landed):
                pool.wait_ge(landed, 16)
                pool.tensor_copy(hi, w)
                pool.drain()
                return pool.tensor_tensor(lo, w, hi.bitcast(F32), ALU.subtract)

            def split_expert(e):
                split(w1[:, e, :].rearrange("d (p c) -> d c p", c=FC), w1h[:, e], w1l[:, e], w1_in[0])\
                    .then_inc(w1_split, 1)
                split(w2[:, e], w2h[:, e], w2l[:, e], w2_in[0]).then_inc(w2_split, 1)

            def power(n):
                for b in range(B):
                    pool.wait_ge(moments_ready, B * n + b + 1)
                    done(pool.tensor_scalar(var_eps[:, b, :], moments[:, b, :, 1], EPS, None, ALU.add))
                    pool.tensor_tensor(rstd[:, b, :], var_eps[:, b, :], minus_half[:, :],
                                       ALU.pow).then_inc(rstd_ready, 1)

            power(0)
            split_expert(0)
            power(1)
            split_expert(1)
            power(2)
            pool.wait_ge(bo1_in, 16)
            for b in range(B):
                pool.wait_ge(xn_ready, 2 * B + b + 1)
                pool.tensor_tensor(x[:, b], x[:, b], bo1[:, :].unsqueeze(1).to_broadcast([P, T, D]),
                                   ALU.add).then_inc(x2b_ready, 1)
            for t in range(B * T):
                pool.wait_ge(r1_ready, t + 1)
                if t >= 2:
                    pool.wait_ge(p1T_psum, t - 1)
                pool.tensor_tensor(probs1[:, t % 2], shifted1[:, t % 2],
                                   small1[:, 2, t % 2, :].unsqueeze(2).to_broadcast([P, H, J]),
                                   ALU.mult).then_inc(p1_ready, 1)
            power(3)
            with pool.Fori(1, E // 2) as it:
                for k in range(2):
                    e = it * 2 + k
                    pool.wait_ge(mm1_done, it * PAIR + (k * FC + FC - PAIR))
                    split(w1[:, bass.ds(e, 1), :].rearrange("d e (p c) -> d (e c) p", c=FC), w1h[:, k],
                          w1l[:, k], w1_in[1]).then_inc(w1_split, 1)
                    pool.wait_ge(mm2_done, it * PAIR + (k * FC + FC - PAIR))
                    split(w2[:, bass.ds(e, 1), :, :].rearrange("p e c d -> p (e c) d"), w2h[:, k],
                          w2l[:, k], w2_in[1]).then_inc(w2_split, 1)

        @block.scalar
        def _(act):
            act.dma_start(wq0[:, :], i["L0_xattn_Wq"]).then_inc(wq0_in, 16)
            act.dma_start(bq0[:, :], column(i["L0_xattn_bq"])).then_inc(wq0_in, 16)
            act.dma_start(wv0[0:C, :], i["L0_xattn_Wv"]).then_inc(kv0_in, 16)
            act.dma_start(wv0[C:C + 1, :], i["L0_xattn_bv"].rearrange("(a d) -> a d", a=1)).then_inc(kv0_in, 16)
            for n, name in enumerate(("bf", "bi", "bc", "bo")):
                act.dma_start(bias_f[:, n:n + 1], column(i["L0_ffn_" + name])).then_inc(ffb_in, 16)
            act.dma_start(in_c[:, :], column(i["L0_ffn_in_c"])).then_inc(ffb_in, 16)
            act.dma_start(wg[:, :], i["L1_ffn_w_gate"]).then_inc(gate_in, 16)
            act.dma_start(b2[:, :], i["L1_ffn_b2"]).then_inc(b2_in, 16)
            act.dma_start(b1[:, :, :], b1_v).then_inc(b1_in, 16)

            def copy(o, x):
                return nc.scalar.activation(o, x, ACT.Copy)

            def evacuate_xnT(n, b):
                act.wait_ge(xnT_psum, B * n + b + 1)
                copy(xnT[:, b, :], bank(b)).then_inc(xnT_ready, 1)

            for b in range(B):
                evacuate_xnT(0, b)
            for b in range(B):
                act.wait_ge(sh0_ready, b + 1)
                nc.scalar.activation(shifted0[:, b], shifted0[:, b], ACT.Exp).then_inc(e0_ready, 1)
            act.wait_ge(turn_psum, 2)
            copy(gate_wT[:, :, :], bank(4)).then_inc(gate_wT_ready, 1)
            act.wait_ge(turn_psum, 3)
            nc.scalar.activation(gate_uT[:, :, :], bank(5), ACT.Copy, scale=0.5).then_inc(gate_wT_ready, 1)
            for b in range(B):
                act.wait_ge(p0T_psum, b + 1)
                copy(probs0T[:, b, :], bank(2 + b)[:, 0:P]).then_inc(p0T_ready, 1)
            for n in range(2):
                act.wait_ge(wq1T_psum, n + 1)
                copy(wq1T[:, 4 * n:4 * n + 4, :], bank(6 + n)).then_inc(wq1T_ready, 1)
            act.wait_ge(kv1_psum, 2)
            act.wait_ge(band_zero, 1)
            v_src = bank(5).rearrange("p (k c b j) -> p c b k j", c=2, b=B, j=J)
            v_dst = v1_band[:, :, :, :, :].rearrange("p (k c) b h j -> p c h b k j", c=2)
            for c in range(2):
                for h2 in range(2):
                    rows = slice(DH * h2, DH * h2 + DH)
                    for b in range(B):
                        last = copy(v_dst[rows, c, 2 * c + h2, b], v_src[rows, c, b])
            last.then_inc(v1_ready, 1)
            for b in range(B):
                evacuate_xnT(1, b)
            act.wait_ge(bias_ready, 1)
            for t in range(2):
                bias = (bias_t0, bias_t1)[t]
                for n in range(3):
                    act.wait_ge(z_psum, 3 * t + n + 1)
                    nc.scalar.activation(gates[:, t, n, :], bank(2 + 3 * t + n), ACT.Tanh, bias=bias[:, n:n + 1],
                                         scale=0.5 if n < 2 else 1.0).then_inc(gates_ready, 1)
            for b in range(B):
                act.wait_ge(ho_psum, b + 1)
                nc.scalar.activation(hT[:, b, :], bank(b), ACT.Tanh, bias=bias_f[:, 3:4]).then_inc(hT_ready, 1)
            for n in range(2):
                act.wait_ge(key1_psum, n + 1)
                copy(key1[:, :, 8 * n:8 * n + 8, :].rearrange("d b h j -> d h b j"),
                     bank(2 + n).rearrange("d (h b j) -> d h b j", b=B, j=J)).then_inc(key1_ready, 1)
            for b in range(B):
                act.wait_ge(val1_psum, b + 1)
                copy(val1[:, b, :, :], bank(4 + b)).then_inc(val1_ready, 1)
            for b in range(B):
                evacuate_xnT(2, b)

            def exp1(t):
                act.wait_ge(sh1_ready, t + 1)
                nc.scalar.activation(shifted1[:, t % 2], shifted1[:, t % 2], ACT.Exp).then_inc(e1_ready, 1)

            exp1(0)
            for t in range(B * T):
                if t + 1 < B * T:
                    exp1(t + 1)
                act.wait_ge(p1T_psum, t + 1)
                if t >= 2:
                    act.wait_ge(o1_step, t - 1)
                copy(probs1T[:, t % 2], bank(5 + t % 2)).then_inc(p1T_ready, 1)
            for b in range(B):
                act.wait_ge(xnT_psum, B * 3 + b + 1)
                copy(xh[:, S * b:S * b + S], bank(b)).then_inc(xnT_ready, 1)
            for b in range(B):
                act.wait_ge(gexp_arg, b + 1)
                nc.scalar.activation(g_shift[:, b], g_shift[:, b], ACT.Exp).then_inc(gexp_ready, 1)
            act.wait_ge(b1_in, 16)

            def pair(it, first):
                for k in range(PAIR):
                    s = it * PAIR + k
                    act.wait_ge(mm1_done, s + 1)
                    if not (first and k < 2):
                        act.wait_ge(lo_done, s - 1)
                    h_in = psum[:, 4 + 2 * (k % 2):6 + 2 * (k % 2), :].rearrange("p a n -> p (a n)")
                    if first:
                        bias = b1[:, k // FC, k % FC:k % FC + 1]
                    else:
                        bias = b1[:, bass.ds(it * 2 + k // FC, 1), k % FC]
                    nc.scalar.activation(hid[:, k % 2, :], h_in, ACT.Gelu, bias=bias).then_inc(gelu_done, 1)
                    act.wait_ge(gelu_done, s + 1)
                    if not (first and k < 4):
                        act.wait_ge(mm2_done, s - 3)
                    copy(hh[:, k % 4, :], hid[:, k % 2, :]).then_inc(hi_done, 1)

            pair(0, True)
            with act.Fori(1, E // 2) as it:
                pair(it, False)

        @block.tensor
        def _(pe):
            def mm(o, lhsT, rhs, start=True, stop=True):
                return nc.tensor.matmul(o, lhsT, rhs, start=start, stop=stop, skip_group_check=True)

            def turn(o, x, k=P):
                return nc.tensor.transpose(o, x, ident[0:k, 0:k])

            def turn_xn(n, b):
                pe.wait_ge(xn_ready, B * n + b + 1)
                for t in range(T):
                    last = turn(bank(b)[:, P * t:P * t + P], xn[:, b, t, :])
                last.then_inc(xnT_psum, 1)

            pe.wait_ge(const_ready, 4)
            pe.wait_ge(ctx_in, 16)
            pe.wait_ge(wq0_in, 32)
            turn(bank(7)[0:C, 0:B * J], ctx_rows[:, :], B * J)
            turn(bank(7)[:, P:2 * P], wq0[:, :]).then_inc(turn_psum, 1)
            pe.wait_ge(ctxT_ready, 1)
            pe.wait_ge(kv0_in, 64)
            mm(bank(6)[:, 0:B * J], wk0[:, :], ctxT[:, :, 0, :])
            for b in range(B):
                last = mm(bank(6)[:, P + P * b:2 * P + P * b], ctxT[:, b, :, :].rearrange("c i j -> c (i j)"), wv0[:, :])
            last.then_inc(kv0_psum, 1)
            pe.wait_ge(k0_ready, 1)
            mm(bank(5)[:, 0:B * J], wq0T[:, :], k0T[:, :, :].rearrange("d b j -> d (b j)")).then_inc(key0_psum, 1)
            for b in range(B):
                turn_xn(0, b)
            pe.wait_ge(key0_ready, 1)
            pe.wait_ge(bq_wide_ready, 1)
            for b in range(B):
                mm(bank(2 + b)[:, 0:P], bq0_wide[:, :], k0T[:, b, :].unsqueeze(1).to_broadcast([D, T, J]), stop=False)
                pe.wait_ge(xnT_ready, b + 1)
                for t in range(T):
                    last = mm(bank(2 + b)[:, J * t:J * t + J], xnT[:, b, P * t:P * t + P], key0[:, b, :], start=False)
                last.then_inc(s0_psum, 1)
            pe.wait_ge(ffn_in, 16 * 8)
            for n in range(8):
                last = turn(bank(4 + n // 4)[:, D * (n % 4):D * (n % 4) + D], gate_w[:, n, :])
                if n % 4 == 3:
                    last.then_inc(turn_psum, 1)
            for b in range(B):
                pe.wait_ge(p0_ready, b + 1)
                turn(bank(2 + b)[:, 0:P], probs0[:, b].rearrange("p i j -> p (i j)")).then_inc(p0T_psum, 1)
            pe.wait_ge(v0_ready, 1)
            for b in range(B):
                pe.wait_ge(p0T_ready, b + 1)
                mm(bank(b), probs0T[:, b, :], v0_band[:, b].rearrange("p i d -> p (i d)")).then_inc(o0_psum, 1)
            pe.wait_ge(gate_wT_ready, 2)
            pe.wait_ge(c0x2_ready, 1)
            pe.wait_ge(gate_in, 16)
            for n in range(3):
                mm(bank(6)[:, n:n + 1], gate_uT[:, n, :], c0x2[:, :])
            turn(bank(6)[:, E:2 * E], wg[:, :], E).then_inc(const_psum, 1)
            pe.wait_ge(wkv1_in, 32)
            for n, w in enumerate((wk1, wv1)):
                for c in range(HC):
                    last = mm(bank(4 + n)[:, B * J * c:B * J * (c + 1)], w[:, c, :], ctxT[0:C, :, 0, :])
                last.then_inc(kv1_psum, 1)
            pe.wait_ge(wq1_in, 16)
            pe.wait_ge(bias_ready, 1)
            for n in range(2):
                for c in range(4):
                    last = turn(bank(6 + n)[:, P * c:P * c + P], wq1[:, 4 * n + c, :])
                last.then_inc(wq1T_psum, 1)
            for b in range(B):
                turn_xn(1, b)
            pe.wait_ge(k1_ready, 1)
            pe.wait_ge(v1_ready, 1)
            pe.wait_ge(wq1T_ready, 2)
            pe.wait_ge(xnT_ready, B + 1)
            for n in range(3):
                mm(bank(2 + n), gate_wT[:, n, :], xnT[:, 0, :]).then_inc(z_psum, 1)
            pe.wait_ge(xnT_ready, B + 2)
            for n in range(3):
                mm(bank(5 + n), gate_wT[:, n, :], xnT[:, 1, :], stop=False)
            for b in range(B):
                mm(bank(b), gate_wT[:, 3, :], xnT[:, b, :], stop=False)
            pe.wait_ge(c_ready, 1)
            for n in range(3):
                mm(bank(5 + n), gate_uT[:, n, :], c1x2[:, :], start=False).then_inc(z_psum, 1)
            for c in range(HC):
                last = mm(bank(2 + c // 4)[:, P * (c % 4):P * (c % 4) + P], wq1T[:, c, :],
                          k1_band[:, c].rearrange("p h n -> p (h n)"))
                if c % 4 == 3:
                    last.then_inc(key1_psum, 1)
            pe.wait_ge(c_ready, 2)
            for b in range(B):
                mm(bank(b), gate_uT[:, 3, :], c2x2[:, :], start=False).then_inc(ho_psum, 1)
            pe.wait_ge(wo1_in, 16)
            for b in range(B):
                for k in range(KC):
                    for c in range(2):
                        last = mm(bank(4 + b)[:, D * k:D * k + D],
                                  v1_band[:, 2 * k + c, b].rearrange("p h j -> p (h j)"), wo1[:, 2 * k + c, :],
                                  start=(c == 0), stop=(c == 1))
                last.then_inc(val1_psum, 1)
            for b in range(B):
                pe.wait_ge(hT_ready, b + 1)
                for t in range(T):
                    last = turn(bank(6 + b)[:, D * t:D * t + D], hT[:, b, P * t:P * t + P])
                last.then_inc(h_psum, 1)
            for b in range(B):
                turn_xn(2, b)

            def scores1(t):
                b, n = t // T, t % T
                pe.wait_ge(xnT_ready, 2 * B + b + 1)
                if t >= 3:
                    pe.wait_ge(sh1_ready, t - 2)
                mm(bank(2 + t % 3), xnT[:, b, P * n:P * n + P],
                   key1[:, b].rearrange("d h j -> d (h j)")).then_inc(s1_psum, 1)

            def turn1(t):
                pe.wait_ge(p1_ready, t + 1)
                if t >= 2:
                    pe.wait_ge(p1T_ready, t - 1)
                for k in range(KC):
                    last = turn(bank(5 + t % 2)[:, P * k:P * k + P],
                                probs1[:, t % 2, HPC * k:HPC * k + HPC, :].rearrange("p h j -> p (h j)"))
                last.then_inc(p1T_psum, 1)

            def attend1(t):
                b, n = t // T, t % T
                pe.wait_ge(p1T_ready, t + 1)
                for k in range(KC):
                    last = mm(bank(7 if b == 0 else 1)[:, D * n:D * n + D], probs1T[:, t % 2, k, :], val1[:, b, k, :],
                              start=(k == 0), stop=(k == KC - 1))
                last.then_inc(o1_step, 1)

            pe.wait_ge(key1_ready, 2)
            pe.wait_ge(val1_ready, B)
            pe.wait_ge(x2_ready, B)
            scores1(0)
            scores1(1)
            for t in range(B * T):
                if t + 2 < B * T:
                    scores1(t + 2)
                turn1(t)
                if t >= 1:
                    attend1(t - 1)
            attend1(B * T - 1)
            for b in range(B):
                turn_xn(3, b)
            for b in range(B):
                pe.wait_ge(xl_ready, b + 1)
                for t in range(T):
                    cols = slice(S * b + P * t, S * b + P * t + P)
                    o = bank(2 + b)[:, E * t:E * t + E]
                    mm(o, xh[:, cols], wgT[:, 0, :], stop=False)
                    mm(o, xh[:, cols], wgT[:, 1, :], start=False, stop=False)
                    last = mm(o, xl[:, cols], wgT[:, 0, :], start=False)
                last.then_inc(logit_psum, 1)

            def three_passes(banks, wh, wl, xh, xl, start, stop):
                for n, (w, x) in enumerate(((wh, xh), (wh, xl), (wl, xh))):
                    for half in range(2):
                        last = mm(bank(banks + half), w, x[:, S * half:S * half + S], start=start and n == 0,
                                  stop=stop and n == 2)
                return last

            def product2(k, e, s):
                if k % FC == 0:
                    pe.wait_ge(w2_split, e + 1)
                    if not isinstance(e, int) or e >= 2:
                        pe.wait_ge(y_used, e * 2 - 2)
                    elif e == 1:
                        pe.wait_ge(acc_ready, B)
                pe.wait_ge(lo_done, s + 1)
                slot = k // FC
                three_passes(2 * slot, w2h[:, slot, k % FC, :], w2l[:, slot, k % FC, :], hh[:, k % 4, :],
                             hl[:, k % 4, :], k % FC == 0, k % FC == FC - 1).then_inc(mm2_done, 1)

            def pair(it, first):
                for k in range(PAIR):
                    s, slot = it * PAIR + k, k // FC
                    if k % FC == 0:
                        pe.wait_ge(w1_split, it * 2 + (slot + 1))
                    if not (first and k < 2):
                        pe.wait_ge(gelu_done, s - 1)
                    three_passes(4 + 2 * (k % 2), w1h[:, slot, k % FC, :], w1l[:, slot, k % FC, :], xh[:, :], xl[:, :],
                                 True, True).then_inc(mm1_done, 1)
                    if first and k == 2:
                        turn_combine()
                    if first and k == 4:
                        output_bias()
                    if k >= LAG:
                        product2(k - LAG, it * 2 + (k - LAG) // FC, s - LAG)
                    elif not first:
                        product2(PAIR + k - LAG, None, s - LAG)

            def turn_combine():
                pe.wait_ge(combine_ready, 1)
                for b in range(B):
                    for t in range(T):
                        last = turn(bank(2 + b)[0:E, P * t:P * t + P], combine[:, b, t, :])
                    last.then_inc(combineT_psum, 1)

            def output_bias():
                pe.wait_ge(combineT_ready, B)
                pe.wait_ge(b2_in, 16)
                for b in range(B):
                    mm(bank(2 + b), b2[:, :], combineT[:, S * b:S * b + S]).then_inc(b2_psum, 1)

            pair(0, True)
            with pe.Fori(1, E // 2) as it:
                pair(it, False)
            for k in range(PAIR - LAG, PAIR):
                product2(k, E - 1, STEPS - PAIR + k)
            for b in range(B):
                pe.wait_ge(sum_ready, B * (E - 1) + b + 1)
                for t in range(T):
                    last = turn(bank(b)[:, D * t:D * t + D], acc[:, S * b + P * t:S * b + P * t + P])
                last.then_inc(y_turned, 1)

        @block.vector
        def _(dve):
            steps = [0]

            def done(ins):
                steps[0] += 1
                ins.then_inc(dve_step, 1)
                dve.wait_ge(dve_step, steps[0])

            v = nc.vector

            def norm_moments(x, n, b):
                for t in range(T):
                    last = v.bn_stats(stats[:, b, t, :], x[:, b, t, :])
                done(last)
                for t in range(T):
                    last = v.bn_aggr(moments[:, b, t, :], stats[:, b, t, :])
                last.then_inc(moments_ready, 1)

            def normalize(x, n, b):
                dve.wait_ge(rstd_ready, B * n + b + 1)
                for t in range(T):
                    last = v.tensor_scalar(xn[:, b, t, :], x[:, b, t, :], moments[:, b, t, 0:1], rstd[:, b, t:t + 1],
                                           ALU.subtract, ALU.mult)
                last.then_inc(xn_ready, 1)

            def wide(a, n):
                return a.unsqueeze(len(a.shape)).to_broadcast([*a.shape, n])

            dve.wait_ge(x_in[0], 16)
            norm_moments(x, 0, 0)
            dve.wait_ge(turn_psum, 1)
            dve.wait_ge(const_ready, 4)
            for b in range(B):
                v.tensor_copy(ctxT[0:C, b], bank(7)[0:C, J * b:J * b + J].unsqueeze(1).to_broadcast([C, T, J]))
            v.tensor_copy(wq0T[:, :], bank(7)[:, P:2 * P]).then_inc(ctxT_ready, 1)
            normalize(x, 0, 0)
            dve.wait_ge(x_in[1], 16)
            norm_moments(x, 0, 1)
            dve.wait_ge(kv0_psum, 1)
            v.tensor_copy(k0T[:, :, :].rearrange("d b j -> d (b j)"), bank(6)[:, 0:B * J]).then_inc(k0_ready, 1)
            normalize(x, 0, 1)
            dve.wait_ge(key0_psum, 1)
            v.tensor_copy(key0[:, :, :].rearrange("d b j -> d (b j)"), bank(5)[:, 0:B * J]).then_inc(key0_ready, 1)
            for b in range(B):
                last = v.tensor_tensor(v0_band[:, b], bank(6)[:, P + P * b:2 * P + P * b].unsqueeze(1).to_broadcast([P, T, D]),
                                       wide(bandmask[:, :], D), ALU.mult)
            last.then_inc(v0_ready, 1)
            dve.wait_ge(ffb_in, 16 * 5)
            v.tensor_scalar(c0x2[:, :], in_c[:, :], 2.0, None, ALU.mult).then_inc(c0x2_ready, 1)
            for b in range(B):
                s = bank(2 + b)[:, 0:P].rearrange("p (i j) -> p i j", j=J)
                dve.wait_ge(s0_psum, b + 1)
                done(v.tensor_reduce(small0[:, 0, b, :], s, X, ALU.max))
                v.tensor_tensor(shifted0[:, b], s, wide(small0[:, 0, b, :], J), ALU.subtract).then_inc(sh0_ready, 1)
            for b in range(B):
                dve.wait_ge(e0_ready, b + 1)
                done(v.tensor_reduce(small0[:, 1, b, :], shifted0[:, b], X, ALU.add))
                done(v.reciprocal(small0[:, 2, b, :], small0[:, 1, b, :]))
                v.tensor_tensor(probs0[:, b], shifted0[:, b], wide(small0[:, 2, b, :], J), ALU.mult).then_inc(p0_ready, 1)
            for b in range(B):
                dve.wait_ge(o0_psum, b + 1)
                done(v.tensor_tensor(x[:, b].rearrange("p i d -> p (i d)"), bank(b),
                                     x[:, b].rearrange("p i d -> p (i d)"), ALU.add))
                norm_moments(x, 1, b)
            for b in range(B):
                normalize(x, 1, b)
            dve.wait_ge(const_psum, 1)
            done(v.tensor_tensor(bias_t0[:, :], bank(6)[:, 0:3], bias_f[:, 0:3], ALU.add))
            v.tensor_scalar(bias_t0[:, 0:2], bias_t0[:, 0:2], 0.5, None, ALU.mult)
            v.tensor_scalar(bias_t1[:, 0:2], bias_f[:, 0:2], 0.5, None, ALU.mult)
            v.tensor_copy(bias_t1[:, 2:3], bias_f[:, 2:3])
            done(v.tensor_copy(wgT[:, 0, :], bank(6)[:, E:2 * E]))
            v.tensor_tensor(wgT[:, 1, :], bank(6)[:, E:2 * E], wgT[:, 0, :].bitcast(F32), ALU.subtract)\
                .then_inc(bias_ready, 1)
            dve.wait_ge(kv1_psum, 1)
            dve.wait_ge(band_zero, 1)
            for h in range(2):
                rows = slice(DH * h, DH * h + DH)
                last = v.tensor_scalar(k1_band[rows, :, h, :], bank(4)[rows, :].rearrange("p (c n) -> p c n", c=HC),
                                       DH ** -0.5, None, ALU.mult)
            last.then_inc(k1_ready, 1)
            dve.wait_ge(gates_ready, 2)
            v.tensor_scalar(keep_c[:, :], gates[:, 0, 0, :], 1.0, in_c[:, 0:1], ALU.add, ALU.mult)
            dve.wait_ge(gates_ready, 3)
            done(v.scalar_tensor_tensor(out=new_c[:, :], in0=gates[:, 0, 1, :], scalar=1.0, in1=gates[:, 0, 2, :],
                                        op0=ALU.add, op1=ALU.mult))
            v.tensor_tensor(c1x2[:, :], keep_c[:, :], new_c[:, :], ALU.add).then_inc(c_ready, 1)
            dve.wait_ge(c_ready, 1)
            dve.wait_ge(gates_ready, 4)
            v.scalar_tensor_tensor(out=keep_c[:, :], in0=gates[:, 1, 0, :], scalar=1.0, in1=c1x2[:, :],
                                   op0=ALU.add, op1=ALU.mult)
            dve.wait_ge(gates_ready, 6)
            done(v.scalar_tensor_tensor(out=new_c[:, :], in0=gates[:, 1, 1, :], scalar=1.0, in1=gates[:, 1, 2, :],
                                        op0=ALU.add, op1=ALU.mult))
            v.scalar_tensor_tensor(out=c2x2[:, :], in0=keep_c[:, :], scalar=0.5, in1=new_c[:, :],
                                   op0=ALU.mult, op1=ALU.add).then_inc(c_ready, 1)
            for b in range(B):
                dve.wait_ge(h_psum, b + 1)
                v.tensor_tensor(x[:, b].rearrange("p i d -> p (i d)"), bank(6 + b),
                                x[:, b].rearrange("p i d -> p (i d)"), ALU.add).then_inc(x2_ready, 1)
                dve.wait_ge(x2_ready, b + 1)
                norm_moments(x, 2, b)
            for b in range(B):
                normalize(x, 2, b)

            def shift1(t):
                s = bank(2 + t % 3).rearrange("p (h j) -> p h j", j=J)
                dve.wait_ge(s1_psum, t + 1)
                done(v.tensor_reduce(small1[:, 0, t % 2, :], s, X, ALU.max))
                if t >= 2:
                    dve.wait_ge(p1_ready, t - 1)
                v.tensor_tensor(shifted1[:, t % 2], s, wide(small1[:, 0, t % 2, :], J), ALU.subtract).then_inc(sh1_ready, 1)

            shift1(0)
            for t in range(B * T):
                if t + 1 < B * T:
                    shift1(t + 1)
                dve.wait_ge(e1_ready, t + 1)
                done(v.tensor_reduce(small1[:, 1, t % 2, :], shifted1[:, t % 2], X, ALU.add))
                v.reciprocal(small1[:, 2, t % 2, :], small1[:, 1, t % 2, :]).then_inc(r1_ready, 1)
            for b in range(B):
                dve.wait_ge(o1_step, T * (b + 1))
                dve.wait_ge(x2b_ready, b + 1)
                done(v.tensor_tensor(x[:, b].rearrange("p i d -> p (i d)"), bank(7 if b == 0 else 1),
                                     x[:, b].rearrange("p i d -> p (i d)"), ALU.add))
                norm_moments(x, 3, b)
            for b in range(B):
                normalize(x, 3, b)
            for b in range(B):
                dve.wait_ge(xnT_ready, 3 * B + b + 1)
                v.tensor_tensor(xl[:, S * b:S * b + S], bank(b), xh[:, S * b:S * b + S].bitcast(F32),
                                ALU.subtract).then_inc(xl_ready, 1)
            for b in range(B):
                s = bank(2 + b)[:, 0:T * E].rearrange("p (i e) -> p i e", e=E)
                dve.wait_ge(logit_psum, b + 1)
                done(v.tensor_reduce(g_small[:, 0, b, :], s, X, ALU.max))
                v.tensor_tensor(g_shift[:, b], s, wide(g_small[:, 0, b, :], E), ALU.subtract).then_inc(gexp_arg, 1)
            dve.wait_ge(gexp_ready, B)
            tiles = "p b i e -> p (b i) e"
            gs, gp, eq = (a[:, :, :, :].rearrange(tiles) for a in (g_shift, g_prob, g_eq))
            first, rest, com = (a[:, :, :, :].rearrange(tiles) for a in (g_first, g_rest, combine))
            sm = [g_small[:, n].rearrange("p b i -> p (b i)") for n in range(4)]
            down = descend[:, :].unsqueeze(1).to_broadcast([P, B * T, E])
            done(v.tensor_reduce(sm[0], gs, X, ALU.add))
            done(v.reciprocal(sm[1], sm[0]))
            done(v.tensor_tensor(gp, gs, wide(sm[1], E), ALU.mult))

            def pick(g, chosen):
                done(v.tensor_reduce(sm[2], g, X, ALU.max))
                done(v.tensor_tensor(eq, g, wide(sm[2], E), ALU.is_equal))
                done(v.tensor_tensor(eq, eq, down, ALU.mult))
                done(v.tensor_reduce(sm[3], eq, X, ALU.max))
                done(v.tensor_tensor(chosen, eq, wide(sm[3], E), ALU.is_equal))

            pick(gp, first)
            done(v.scalar_tensor_tensor(out=rest, in0=first, scalar=-2.0, in1=gp, op0=ALU.mult, op1=ALU.add))
            pick(rest, com)
            done(v.tensor_tensor(eq, com, first, ALU.add))
            v.tensor_tensor(com, eq, gp, ALU.mult).then_inc(combine_ready, 1)

            def weigh(half, slot, e):
                cols = slice(S * half, S * half + S)
                dve.wait_ge(mm2_done, e * FC + FC)
                dve.wait_ge(cwb_in[0], 16)
                if not isinstance(e, int) or e >= 2:
                    dve.wait_ge(cwb_in[1], 16)
                w = cwb[:, e, cols] if isinstance(e, int) else cwb[:, bass.ds(e, 1), cols].rearrange("p e n -> p (e n)")
                if not isinstance(e, int) or e >= 1:
                    dve.wait_ge(sum_ready, e * 2 + (half - 1))
                v.tensor_tensor(part[:, half], bank(2 * slot + half), w, ALU.mult).then_inc(y_used, 1)
                dve.wait_ge(y_used, e * 2 + (half + 1))
                v.tensor_tensor(acc[:, cols], acc[:, cols], part[:, half], ALU.add).then_inc(sum_ready, 1)

            def pair(it, first):
                for k in range(PAIR):
                    s = it * PAIR + k
                    dve.wait_ge(hi_done, s + 1)
                    if not (first and k < 4):
                        dve.wait_ge(mm2_done, s - 3)
                    v.tensor_tensor(hl[:, k % 4, :], hid[:, k % 2, :], hh[:, k % 4, :].bitcast(F32),
                                    ALU.subtract).then_inc(lo_done, 1)
                    if first and k == 0:
                        for b in range(B):
                            dve.wait_ge(combineT_psum, b + 1)
                            v.tensor_copy(combineT[:, S * b:S * b + S], bank(2 + b)[0:E, :]).then_inc(combineT_ready, 1)
                    if first and k == 3:
                        for b in range(B):
                            dve.wait_ge(b2_psum, b + 1)
                            v.tensor_copy(acc[:, S * b:S * b + S], bank(2 + b)).then_inc(acc_ready, 1)
                    if k % FC in (1, 2) and not (first and k < FC):
                        weigh(k % FC - 1, (k // FC + 1) % 2, it * 2 + (k // FC - 1))

            pair(0, True)
            with dve.Fori(1, E // 2) as it:
                pair(it, False)
            for half in range(2):
                weigh(half, 1, E - 1)
            for b in range(B):
                dve.wait_ge(y_turned, b + 1)
                v.tensor_tensor(x[:, b].rearrange("p i d -> p (i d)"), bank(b),
                                x[:, b].rearrange("p i d -> p (i d)"), ALU.add).then_inc(res_ready, 1)


NAMES = ['x', 'ctx_768', 'L0_xattn_Wq', 'L0_xattn_bq', 'L0_xattn_Wk', 'L0_xattn_bk', 'L0_xattn_Wv', 'L0_xattn_bv',
         'L0_ffn_wf', 'L0_ffn_uf', 'L0_ffn_bf', 'L0_ffn_wi', 'L0_ffn_ui', 'L0_ffn_bi', 'L0_ffn_wc', 'L0_ffn_uc',
         'L0_ffn_bc', 'L0_ffn_wo', 'L0_ffn_uo', 'L0_ffn_bo', 'L0_ffn_in_c', 'L1_xattn_w_q', 'L1_xattn_w_k',
         'L1_xattn_w_v', 'L1_xattn_w_o', 'L1_xattn_b_o', 'L1_ffn_w_gate', 'L1_ffn_W1', 'L1_ffn_b1', 'L1_ffn_W2',
         'L1_ffn_b2']


def kernel(**inputs):
    import numpy as np
    import concourse.bacc as bacc
    from concourse.bass_utils import run_bass_kernel_spmd

    nc = bacc.Bacc("TRN2", target_bir_lowering=False, num_devices=1)
    arrays, views = {}, {}
    for name in NAMES:
        a = np.ascontiguousarray(inputs[name])
        arrays[f"in_{name}"] = a
        views[name] = nc.dram_tensor(f"in_{name}", a.shape, mybir.dt.from_np(a.dtype), kind="ExternalInput").ap()
    out = nc.dram_tensor("out_x", (B, S, D), F32, kind="ExternalOutput").ap()
    two_layers(nc, views, out)
    r = run_bass_kernel_spmd(nc, [arrays], core_ids=[0])
    return r.results[0]["out_x"]
```

```python
from contextlib import ExitStack

import concourse.bass as bass
from concourse import mybir

F32 = mybir.dt.float32
F32R = mybir.dt.float32r
ALU = mybir.AluOpType
ACT = mybir.ActivationFunctionType
X = mybir.AxisListType.X

P = 128
B = 2
S = 512
T = S // P
D = 128
C = 96
J = 32
H = 16
DH = 64
HC = H * DH // P
KC = H * J // P
HPC = P // J
E = 8
F = 512
FC = F // P
LAG = 2
PAIR = 2 * FC
EPS = 1e-5
LOWEST = -3e38
WARM_UP = 8

PACK0 = [("ctxT", B * J), ("wq0", D), ("wk0", D), ("wv0", D), ("centre", D), ("bq0", 1)]
PACK1 = [("ident", P), ("bandmask", T), ("descend", E), ("minus_half", T), ("euler", T * E), ("bias_f", 4),
         ("in_c", 1), ("wgT", E), ("b1", E * FC), ("b2T", E)]

ROUTER0, TURN1, ROUTER1 = 1, 4, 7
XH1 = 4
SHIFT0, X_LO1, SHIFT1 = 2, 5, 7


def two_layers(nc, i, out):
    ctx = ExitStack()
    with ctx:
        def sb(name, shape, dt=F32):
            return ctx.enter_context(nc.sbuf_tensor(name, shape, dt))

        def sem(name):
            return ctx.enter_context(nc.semaphore(name))

        psum = ctx.enter_context(nc.psum_tensor("psum", [P, 8, 512], F32))

        def bank(n):
            return psum[:, n, :]

        def overlay(name, shapes, whole):
            words = whole[1]
            for d in whole[2:]:
                words *= d
            space, at, views = sb(name, [P, words]), 0, []
            for shape in [whole, *shapes]:
                n = 1
                for d in shape[1:]:
                    n *= d
                start = 0 if shape is whole else at
                at = at if shape is whole else at + n
                assert at <= words
                names = " ".join("abcd"[:len(shape) - 1])
                sizes = dict(zip("bcd", shape[2:]))
                views.append(space[0:shape[0], start:start + n].rearrange(f"p ({names}) -> p {names}", **sizes))
            return views

        def packed(name, parts):
            space, at, views = sb(name, [P, sum(n for _, n in parts)]), 0, {}
            for part, n in parts:
                views[part] = space[:, at:at + n]
                at += n
            return space, views

        x = sb("x", [P, B, T, D])
        xn = sb("xn", [P, B, T, D])
        xT = sb("xT", [D, B, S])
        stats = sb("stats", [P, B, T, 6])
        moments = sb("moments", [P, B, T, 2])
        var_eps = sb("var_eps", [P, B, T])
        rstd = sb("rstd", [P, B, T])

        setup0, v0 = packed("setup0", PACK0)
        ctxT, wq0, wk0, wv0 = (v0[n] for n in ("ctxT", "wq0", "wk0", "wv0"))
        centre, bq0 = v0["centre"], v0["bq0"]
        setup1, v1 = packed("setup1", PACK1)
        ident, bandmask, descend = v1["ident"], v1["bandmask"], v1["descend"]
        minus_half, euler, bias_f, in_c = v1["minus_half"], v1["euler"], v1["bias_f"], v1["in_c"]
        wgT_in, b2T, b1 = v1["wgT"], v1["b2T"], v1["b1"].rearrange("p (e c) -> p e c", c=FC)

        ctx_rep = sb("ctx_rep", [C + 1, B, T, J])
        wq0T = sb("wq0T", [D, D])
        bq0_wide = sb("bq0_wide", [D, P])
        k0T = sb("k0T", [D, B, J])
        v0_band = sb("v0_band", [P, B, T, D])
        key0 = sb("key0", [D, B, J])
        bias0 = sb("bias0", [P, B, J])

        gate_T = sb("gate_T", [D, 8, D])
        gate_uT = sb("gate_uT", [D, 4, D])
        c0x2 = sb("c0x2", [D, 1])
        bias_t0 = sb("bias_t0", [D, 3])
        bias_t1 = sb("bias_t1", [D, 3])

        wq1T = sb("wq1T", [P, HC, D])
        k1_band = sb("k1_band", [P, HC, 2, B * J])
        bo1 = sb("bo1", [P, D])
        key1 = sb("key1", [D, B, H, J])
        val1 = sb("val1", [P, B, KC, D])

        raw0 = sb("raw0", [P, B, T, J])
        shifted0 = sb("shifted0", [P, B, T, J])
        probs0 = sb("probs0", [P, B, T, J])
        probs0T = sb("probs0T", [P, B, P])
        small0 = sb("small0", [P, 3, B, T])
        shifted1 = sb("shifted1", [P, 3, H, J])
        probs1 = sb("probs1", [P, 2, H, J])
        probs1T = sb("probs1T", [P, 2, KC, P])
        small1 = sb("small1", [P, 3, 3, H])

        table_in = sb("table_in", [P, 1])
        wgT = sb("wgT", [D, 2, E], F32R)
        xh = sb("xh", [D, B * S], F32R)
        xl = sb("xl", [D, B * S], F32R)
        g_shift = sb("g_shift", [P, B * T, E])
        g_prob = sb("g_prob", [P, B * T, E])
        g_small = sb("g_small", [P, 4, B * T])
        g_eq = sb("g_eq", [P, B * T, E])
        g_first = sb("g_first", [P, B * T, E])
        g_rest = sb("g_rest", [P, B * T, E])
        combine = sb("combine", [P, B * T, E])
        combineT = sb("combineT", [E, B * S])
        cwb, gates, keep_c, new_c, c1x2, c2x2, hT, v1_band = overlay("cwb", [
            [D, 2, 3, S], [D, S], [D, S], [D, S], [D, S], [D, B, S], [P, HC, B, HPC, J]], [P, E, B * S])
        hid, wk1, wv1 = overlay("hid", [[C, HC, P], [C, HC, P]], [P, 2, B * S])
        part, wo1 = overlay("part", [[P, HC, D]], [P, 2, S])
        acc, wq1 = overlay("acc", [[D, HC, P]], [D, B * S])
        combine_dram = nc.dram_tensor("combine_dram", [E, B * S], F32, kind="Internal").ap()

        w1 = sb("w1", [D, E, FC, P])
        w2 = sb("w2", [P, E, FC, D])
        w1h = sb("w1h", [D, 2, FC, P], F32R)
        w1l = sb("w1l", [D, 2, FC, P], F32R)
        w2h = sb("w2h", [P, 2, FC, D], F32R)
        w2l = sb("w2l", [P, 2, FC, D], F32R)
        hh = sb("hh", [P, 4, B * S], F32R)
        hl = sb("hl", [P, 4, B * S], F32R)
        hid_half = hid.rearrange("p a (b n) -> p (a b) n", b=B)
        hh_half = hh[:, :, :].rearrange("p a (b n) -> p (a b) n", b=B)
        hl_half = hl[:, :, :].rearrange("p a (b n) -> p (a b) n", b=B)

        x_in, w1_in, w2_in = ([sem(f"{a}_in{n}") for n in range(2)] for a in ("x", "w1", "w2"))
        cwb_in = [sem(f"cwb_in{n}") for n in range(3)]
        (setup0_in, setup1_in, xT_in, gate_in, wq1_in, wkv1_in, wo1_in, bo1_in, combine_out, out_done) = (
            sem(n) for n in ("setup0_in", "setup1_in", "xT_in", "gate_in", "wq1_in", "wkv1_in", "wo1_in", "bo1_in",
                             "combine_out", "out_done"))
        zeros_ready = sem("zeros_ready")
        dve_step, pool_step = sem("dve_step"), sem("pool_step")
        bq_wide_ready, ctx_rep_ready, gate_uT_ready = sem("bq_wide_ready"), sem("ctx_rep_ready"), sem("gate_uT_ready")
        wq0T_psum, wq0T_ready = sem("wq0T_psum"), sem("wq0T_ready")
        const_psum, bias_ready, c0x2_ready = sem("const_psum"), sem("bias_ready"), sem("c0x2_ready")
        kv0_psum, k0_ready, v0_ready = sem("kv0_psum"), sem("k0_ready"), sem("v0_ready")
        key0_psum, key0_ready = sem("key0_psum"), sem("key0_ready")
        wq1T_psum, wq1T_ready, band_zero = sem("wq1T_psum"), sem("wq1T_ready"), sem("band_zero")
        kv1_psum, k1_ready, v1_ready = sem("kv1_psum"), sem("k1_ready"), sem("v1_ready")
        key1_psum, key1_ready = sem("key1_psum"), sem("key1_ready")
        val1_psum, val1_ready = sem("val1_psum"), sem("val1_ready")
        moments_ready, rstd_ready, xn_ready = sem("moments_ready"), sem("rstd_ready"), sem("xn_ready")
        xT_psum, xT_ready = sem("xT_psum"), sem("xT_ready")
        s0_psum, sh0_ready, e0_ready, p0_ready = sem("s0_psum"), sem("sh0_ready"), sem("e0_ready"), sem("p0_ready")
        p0T_psum, p0T_ready, o0_psum = sem("p0T_psum"), sem("p0T_ready"), sem("o0_psum")
        z_psum, gates_ready, c_ready = sem("z_psum"), sem("gates_ready"), sem("c_ready")
        ho_psum, hT_ready, h_psum = sem("ho_psum"), sem("hT_ready"), sem("h_psum")
        x2_ready, x2b_ready = sem("x2_ready"), sem("x2b_ready")
        s1_psum, max1_done, sh1_ready, e1_ready = sem("s1_psum"), sem("max1_done"), sem("sh1_ready"), sem("e1_ready")
        sum1_done, r1_ready, p1_ready = sem("sum1_done"), sem("r1_ready"), sem("p1_ready")
        p1T_psum, p1T_ready, o1_step = sem("p1T_psum"), sem("p1T_ready"), sem("o1_step")
        xl_ready, logit_psum, gexp_arg, gexp_ready = sem("xl_ready"), sem("logit_psum"), sem("gexp_arg"), sem("gexp_ready")
        combine_ready, combineT_psum, combineT_ready = sem("combine_ready"), sem("combineT_psum"), sem("combineT_ready")
        w1_split, w2_split = sem("w1_split"), sem("w2_split")
        mm1_done, mm2_done = sem("mm1_done"), sem("mm2_done")
        gelu_done, hi_done, lo_done = sem("gelu_done"), sem("hi_done"), sem("lo_done")
        last_y, y_used, sum_ready, y_turned, res_ready = sem("last_y"), sem("y_used"), sem("sum_ready"), sem("y_turned"), sem("res_ready")

        x_v = i["x"].rearrange("b (p i) d -> b p i d", i=T)
        out_v = out.rearrange("b (p i) d -> b p i d", i=T)

        block = ctx.enter_context(nc.Block())

        @block.sync
        def _(sp):
            sp.dma_start(xT[:, :, :], i["xT"]).then_inc(xT_in, 16)
            for b in range(B):
                sp.dma_start(x[:, b], x_v[b]).then_inc(x_in[b], 16)
            sp.dma_start(gate_T[:, :, :], i["gate_T"]).then_inc(gate_in, 16)
            sp.dma_start(wq1[:, :, :], i["wq1"]).then_inc(wq1_in, 16)
            sp.dma_start(wo1[:, :, :], i["wo1"]).then_inc(wo1_in, 16)
            sp.dma_start(w1[:, 0:2], i["w1"][:, 0:2]).then_inc(w1_in[0], 16)
            sp.dma_start(w2[:, 0:2], i["w2"][:, 0:2]).then_inc(w2_in[0], 16)
            sp.dma_start(w1[:, 2:E], i["w1"][:, 2:E]).then_inc(w1_in[1], 16)
            sp.dma_start(w2[:, 2:E], i["w2"][:, 2:E]).then_inc(w2_in[1], 16)
            sp.wait_ge(combineT_ready, B)
            sp.dma_start(combine_dram, combineT[:, :]).then_inc(combine_out, 16)
            sp.wait_ge(combine_out, 16)
            for n, (e, m) in enumerate(((0, 1), (1, 1), (2, E - 2))):
                sp.dma_start(cwb[:, e:e + m, :], combine_dram[e:e + m, :].partition_broadcast(P)).then_inc(cwb_in[n], 16)
            for b in range(B):
                sp.wait_ge(res_ready, b + 1)
                sp.dma_start(out_v[b], x[:, b]).then_inc(out_done, 16)
            sp.wait_ge(out_done, 16 * B)

        @block.gpsimd
        def _(pool):
            steps = [0]

            def done(ins):
                steps[0] += 1
                ins.then_inc(pool_step, 1)
                pool.wait_ge(pool_step, steps[0])

            def split(w, hi, lo, landed):
                pool.wait_ge(landed, 16)
                pool.tensor_copy(hi, w)
                pool.drain()
                return pool.tensor_tensor(lo, w, hi.bitcast(F32), ALU.subtract)

            def power(n, b):
                pool.wait_ge(moments_ready, B * n + b + 1)
                done(pool.tensor_scalar(var_eps[:, b, :], moments[:, b, :, 1], EPS, None, ALU.add))
                pool.tensor_tensor(rstd[:, b, :], var_eps[:, b, :], minus_half, ALU.pow).then_inc(rstd_ready, 1)

            pool.wait_ge(setup0_in, 16)
            pool.tensor_scalar(bq0_wide[:, :], centre, 0.0, bq0, ALU.mult, ALU.add).then_inc(bq_wide_ready, 1)
            pool.wait_ge(setup1_in, 16)
            for b in range(B):
                power(0, b)
            for e in range(2):
                for b in range(B):
                    if e == 1:
                        power(1, b)
                split(w1[:, e], w1h[:, e], w1l[:, e], w1_in[0]).then_inc(w1_split, 1)
                split(w2[:, e], w2h[:, e], w2l[:, e], w2_in[0]).then_inc(w2_split, 1)
            pool.wait_ge(bo1_in, 16)
            for b in range(B):
                power(2, b)
            for b in range(B):
                pool.wait_ge(xT_psum, B + b + 1)
                pool.tensor_tensor(x[:, b], x[:, b], bo1[:, :].unsqueeze(1).to_broadcast([P, T, D]),
                                   ALU.add).then_inc(x2b_ready, 1)
            for t in range(B * T):
                if t == 6:
                    power(3, 0)
                pool.wait_ge(r1_ready, t + 1)
                if t >= 2:
                    pool.wait_ge(p1T_psum, t - 1)
                pool.tensor_tensor(probs1[:, t % 2], shifted1[:, t % 3],
                                   small1[:, 2, t % 3, :].unsqueeze(2).to_broadcast([P, H, J]),
                                   ALU.mult).then_inc(p1_ready, 1)
            power(3, 1)
            for b in range(B):
                pool.wait_ge(gexp_arg, b + 1)
                gs, gp = (a[:, T * b:T * b + T, :].rearrange("p t e -> p (t e)") for a in (g_shift, g_prob))
                pool.tensor_tensor(gp, euler, gs, ALU.pow).then_inc(gexp_ready, 1)
            with pool.Fori(2, E // 2 + 1) as it:
                for k in range(2):
                    e = it * 2 + (k - 2)
                    pool.wait_ge(mm1_done, it * PAIR + (k * FC - FC))
                    split(w1[:, bass.ds(e, 1), :, :].rearrange("d e c p -> d (e c) p"), w1h[:, k], w1l[:, k],
                          w1_in[1]).then_inc(w1_split, 1)
                    pool.wait_ge(mm2_done, it * PAIR + (k * FC - FC))
                    split(w2[:, bass.ds(e, 1), :, :].rearrange("p e c d -> p (e c) d"), w2h[:, k], w2l[:, k],
                          w2_in[1]).then_inc(w2_split, 1)

        @block.scalar
        def _(act):
            act.dma_start(setup0[:, :], i["setup0"]).then_inc(setup0_in, 16)
            act.dma_start(setup1[:, :], i["setup1"]).then_inc(setup1_in, 16)
            act.dma_start(wk1, i["wk1"]).then_inc(wkv1_in, 16)
            act.dma_start(wv1, i["wv1"]).then_inc(wkv1_in, 16)
            act.dma_start(bo1[:, :], i["bo1"].partition_broadcast(P)).then_inc(bo1_in, 16)

            def copy(o, x):
                return nc.scalar.activation(o, x, ACT.Copy)

            def evacuate_xT(n, b):
                act.wait_ge(xT_psum, B * (n - 1) + b + 1)
                copy(xT[:, b, :], bank(b)).then_inc(xT_ready, 1)

            for b in range(B):
                act.wait_ge(sh0_ready, b + 1)
                nc.scalar.activation(shifted0[:, b], shifted0[:, b], ACT.Exp).then_inc(e0_ready, 1)
            act.wait_ge(gate_in, 16)
            nc.scalar.activation(gate_uT[:, :, :], gate_T[:, 4:8, :], ACT.Copy, scale=0.5).then_inc(gate_uT_ready, 1)
            for b in range(B):
                act.wait_ge(p0T_psum, b + 1)
                copy(probs0T[:, b, :], bank(2 + b)[:, 0:P]).then_inc(p0T_ready, 1)
            act.wait_ge(kv1_psum, 1)
            act.wait_ge(band_zero, 1)
            v_src = bank(7).rearrange("p (k c b j) -> p c b k j", c=2, b=B, j=J)
            v_dst = v1_band.rearrange("p (k c) b h j -> p c h b k j", c=2)
            for c in range(2):
                for h2 in range(2):
                    rows = slice(DH * h2, DH * h2 + DH)
                    for b in range(B):
                        last = copy(v_dst[rows, c, 2 * c + h2, b], v_src[rows, c, b])
            last.then_inc(v1_ready, 1)
            for n in range(2):
                act.wait_ge(wq1T_psum, n + 1)
                copy(wq1T[:, 4 * n:4 * n + 4, :], bank(6 + n)).then_inc(wq1T_ready, 1)
            for b in range(B):
                evacuate_xT(1, b)
            act.wait_ge(bias_ready, 1)

            def gate(t, n):
                act.wait_ge(z_psum, 3 * t + n + 1)
                nc.scalar.activation(gates[:, t, n, :], bank(2 + 3 * t + n), ACT.Tanh,
                                     bias=(bias_t0, bias_t1)[t][:, n:n + 1],
                                     scale=0.5 if n < 2 else 1.0).then_inc(gates_ready, 1)

            def evacuate_val1(b):
                act.wait_ge(val1_psum, b + 1)
                copy(val1[:, b, :, :], bank(4 + b)).then_inc(val1_ready, 1)

            for n in range(3):
                gate(0, n)
            for n in range(2):
                act.wait_ge(key1_psum, n + 1)
                copy(key1[:, :, 8 * n:8 * n + 8, :].rearrange("d b h j -> d h b j"),
                     bank(2 + n).rearrange("d (h b j) -> d h b j", b=B, j=J)).then_inc(key1_ready, 1)
            for n in range(3):
                gate(1, n)
            evacuate_val1(0)
            for b in range(B):
                act.wait_ge(ho_psum, b + 1)
                nc.scalar.activation(hT[:, b, :], bank(b), ACT.Tanh, bias=bias_f[:, 3:4]).then_inc(hT_ready, 1)
            evacuate_xT(2, 0)
            evacuate_val1(1)
            evacuate_xT(2, 1)

            def exp1(t):
                act.wait_ge(sh1_ready, t + 1)
                act.wait_ge(rstd_ready, 2 * B + t // T + 1)
                nc.scalar.activation(shifted1[:, t % 3], shifted1[:, t % 3], ACT.Exp,
                                     scale=rstd[:, t // T, t % T:t % T + 1]).then_inc(e1_ready, 1)

            def evacuate_xh(b):
                act.wait_ge(xT_psum, 2 * B + b + 1)
                copy(xh[:, S * b:S * b + S], bank(b)).then_inc(xT_ready, 1)

            exp1(0)
            exp1(1)
            for t in range(B * T):
                if t + 2 < B * T:
                    exp1(t + 2)
                if t == 6:
                    nc.scalar.activation(table_in[:, :], b1[:, 0, 0:1], ACT.Gelu)
                if t == 7:
                    evacuate_xh(0)
                act.wait_ge(p1T_psum, t + 1)
                if t >= 2:
                    act.wait_ge(o1_step, t - 1)
                copy(probs1T[:, t % 2], bank(6 - t % 2)).then_inc(p1T_ready, 1)

            for u in range(2 * PAIR):
                k = u % PAIR
                act.wait_ge(mm1_done, u + 1)
                if u >= 4:
                    act.wait_ge(lo_done, u - 3)
                nc.scalar.activation(hid_half[:, u % 4, :], bank(6 + u % 2), ACT.Gelu,
                                     bias=b1[:, k // FC, k % FC:k % FC + 1]).then_inc(gelu_done, 1)
                act.wait_ge(gelu_done, u + 1)
                if u >= 8:
                    act.wait_ge(mm2_done, u - 7)
                copy(hh_half[:, u % 8, :], hid_half[:, u % 4, :]).then_inc(hi_done, 1)
                if u == XH1:
                    evacuate_xh(1)
            with act.Fori(2, E // 2 + 1) as it:
                for k in range(PAIR):
                    u = it * PAIR + k
                    act.wait_ge(mm1_done, u + 1)
                    act.wait_ge(lo_done, u - 1)
                    h_in = psum[:, 6 - 2 * (k % 2):8 - 2 * (k % 2), :].rearrange("p a n -> p (a n)")
                    nc.scalar.activation(hid[:, k % 2, :], h_in, ACT.Gelu,
                                         bias=b1[:, bass.ds(it * 2 + (k // FC - 2), 1), k % FC]).then_inc(gelu_done, 1)
                    act.wait_ge(gelu_done, u + 1)
                    act.wait_ge(mm2_done, u - 3)
                    copy(hh[:, k % 4, :], hid[:, k % 2, :]).then_inc(hi_done, 1)

        @block.tensor
        def _(pe):
            def mm(o, lhsT, rhs, start=True, stop=True):
                return nc.tensor.matmul(o, lhsT, rhs, start=start, stop=stop, skip_group_check=True)

            def turn(o, x, k=P):
                return nc.tensor.transpose(o, x, ident[0:k, 0:k])

            def turn_x(src, b):
                for t in range(T):
                    last = turn(bank(b)[:, P * t:P * t + P], src[:, b, t, :])
                last.then_inc(xT_psum, 1)

            pe.wait_ge(zeros_ready, 1)
            for _ in range(WARM_UP):
                mm(bank(0)[:, 0:P], xn[:, 0, 0, :], xn[:, 0, 0, :])
            pe.wait_ge(setup0_in, 16)
            mm(bank(7)[:, 0:D], wq0, centre).then_inc(wq0T_psum, 1)
            mm(bank(6)[:, 0:B * J], wk0[0:C + 1, :], ctxT[0:C + 1, :]).then_inc(kv0_psum, 1)
            pe.wait_ge(k0_ready, 1)
            pe.wait_ge(bq_wide_ready, 1)
            k0 = k0T[:, :, :].rearrange("d b j -> d (b j)")
            mm(bank(5)[:, 0:B * J], wq0T[:, :], k0)
            mm(bank(5)[:, B * J:2 * B * J], bq0_wide[:, :], k0).then_inc(key0_psum, 1)
            pe.wait_ge(ctx_rep_ready, 1)
            for b in range(B):
                last = mm(bank(4)[:, P * b:P * b + P], ctx_rep[:, b, :, :].rearrange("c i j -> c (i j)"), wv0[0:C + 1, :])
            last.then_inc(kv0_psum, 1)
            pe.wait_ge(key0_ready, 1)
            pe.wait_ge(xT_in, 16)
            for b in range(B):
                for t in range(T):
                    last = mm(bank(2 + b)[:, J * t:J * t + J], xT[:, b, P * t:P * t + P], key0[:, b, :])
                last.then_inc(s0_psum, 1)

            def keys_values1(n, w):
                pe.wait_ge(wkv1_in, 32)
                for c in range(HC):
                    last = mm(bank(n)[:, B * J * c:B * J * (c + 1)], w[:, c, :], ctxT[0:C, :])
                last.then_inc(kv1_psum, 1)

            keys_values1(7, wv1)
            pe.wait_ge(setup1_in, 16)
            for b in range(B):
                pe.wait_ge(p0_ready, b + 1)
                turn(bank(2 + b)[:, 0:P], probs0[:, b].rearrange("p i j -> p (i j)")).then_inc(p0T_psum, 1)
            for b in range(B):
                pe.wait_ge(p0T_ready, b + 1)
                pe.wait_ge(v0_ready, b + 1)
                mm(bank(b), probs0T[:, b, :], v0_band[:, b].rearrange("p i d -> p (i d)")).then_inc(o0_psum, 1)
            pe.wait_ge(gate_uT_ready, 1)
            pe.wait_ge(c0x2_ready, 1)
            for n in range(3):
                last = mm(bank(2)[:, n:n + 1], gate_uT[:, n, :], c0x2[:, :])
            last.then_inc(const_psum, 1)
            keys_values1(5, wk1)
            pe.wait_ge(wq1_in, 16)
            pe.wait_ge(v1_ready, 1)
            for n in range(2):
                for c in range(4):
                    last = mm(bank(6 + n)[:, P * c:P * c + P], wq1[:, 4 * n + c, :], centre)
                last.then_inc(wq1T_psum, 1)
            for b in range(B):
                pe.wait_ge(xn_ready, b + 1)
                turn_x(xn, b)
            pe.wait_ge(bias_ready, 1)
            pe.wait_ge(xT_ready, 1)
            for n in range(3):
                mm(bank(2 + n), gate_T[:, n, :], xT[:, 0, :]).then_inc(z_psum, 1)
            pe.wait_ge(k1_ready, 1)
            pe.wait_ge(wq1T_ready, 2)
            pe.wait_ge(xT_ready, 2)
            for n in range(3):
                mm(bank(5 + n), gate_T[:, n, :], xT[:, 1, :], stop=False)
            for b in range(B):
                mm(bank(b), gate_T[:, 3, :], xT[:, b, :], stop=False)
            pe.wait_ge(gates_ready, 2)
            for c in range(HC):
                last = mm(bank(2 + c // 4)[:, P * (c % 4):P * (c % 4) + P], wq1T[:, c, :],
                          k1_band[:, c].rearrange("p h n -> p (h n)"))
                if c % 4 == 3:
                    last.then_inc(key1_psum, 1)
            pe.wait_ge(c_ready, 1)
            for n in range(3):
                mm(bank(5 + n), gate_uT[:, n, :], c1x2, start=False).then_inc(z_psum, 1)

            def values1(b):
                for k in range(KC):
                    for c in range(2):
                        last = mm(bank(4 + b)[:, D * k:D * k + D],
                                  v1_band[:, 2 * k + c, b].rearrange("p h j -> p (h j)"), wo1[:, 2 * k + c, :],
                                  start=(c == 0), stop=(c == 1))
                last.then_inc(val1_psum, 1)

            pe.wait_ge(wo1_in, 16)
            values1(0)
            pe.wait_ge(c_ready, 2)
            for b in range(B):
                mm(bank(b), gate_uT[:, 3, :], c2x2, start=False).then_inc(ho_psum, 1)
            for b in range(B):
                pe.wait_ge(hT_ready, b + 1)
                for t in range(T):
                    last = turn(bank(6 + b)[:, D * t:D * t + D], hT[:, b, P * t:P * t + P])
                last.then_inc(h_psum, 1)
            values1(1)
            for b in range(B):
                pe.wait_ge(x2_ready, b + 1)
                turn_x(x, b)

            def scores1(t):
                b, n = t // T, t % T
                pe.wait_ge(xT_ready, B + b + 1)
                if t >= 3:
                    pe.wait_ge(sh1_ready, t - 2)
                mm(bank(2 + t % 3), xT[:, b, P * n:P * n + P],
                   key1[:, b].rearrange("d h j -> d (h j)")).then_inc(s1_psum, 1)

            def turn1(t):
                pe.wait_ge(p1_ready, t + 1)
                if t >= 2:
                    pe.wait_ge(p1T_ready, t - 1)
                for k in range(KC):
                    last = turn(bank(6 - t % 2)[:, P * k:P * k + P],
                                probs1[:, t % 2, HPC * k:HPC * k + HPC, :].rearrange("p h j -> p (h j)"))
                last.then_inc(p1T_psum, 1)

            def attend1(t):
                b, n = t // T, t % T
                pe.wait_ge(p1T_ready, t + 1)
                for k in range(KC):
                    last = mm(bank(7 if b == 0 else 1)[:, D * n:D * n + D], probs1T[:, t % 2, k, :], val1[:, b, k, :],
                              start=(k == 0), stop=(k == KC - 1))
                last.then_inc(o1_step, 1)

            pe.wait_ge(key1_ready, 2)
            pe.wait_ge(val1_ready, B)
            for t in range(3):
                scores1(t)
            for t in range(B * T):
                if t + 3 < B * T:
                    scores1(t + 3)
                if t == 7:
                    pe.wait_ge(xn_ready, B + 1)
                    turn_x(xn, 0)
                if t >= 1:
                    attend1(t - 1)
                turn1(t)

            def three_passes(banks, wh, wl, xh, xl, start, stop):
                for n, (w, x) in enumerate(((wh, xh), (wh, xl), (wl, xh))):
                    for half, o in enumerate(banks):
                        last = mm(bank(o), w, x[:, S * half:S * half + S], start=start and n == 0, stop=stop and n == 2)
                return last

            def router(b):
                pe.wait_ge(xl_ready, b + 1)
                for t in range(T):
                    cols = slice(S * b + P * t, S * b + P * t + P)
                    o = bank(3)[:, E * (T * b + t):E * (T * b + t) + E]
                    mm(o, xh[:, cols], wgT[:, 0, :], stop=False)
                    mm(o, xh[:, cols], wgT[:, 1, :], start=False, stop=False)
                    last = mm(o, xl[:, cols], wgT[:, 0, :], start=False)
                last.then_inc(logit_psum, 1)

            def turn_combine():
                pe.wait_ge(combine_ready, 1)
                for b in range(B):
                    for t in range(T):
                        last = turn(bank(4 + b)[0:E, P * t:P * t + P], combine[:, T * b + t, :])
                    last.then_inc(combineT_psum, 1)

            def half_product1(u):
                half, k = u // PAIR, u % PAIR
                if k == 0:
                    pe.wait_ge(xl_ready, half + 1)
                if k % FC == 0:
                    pe.wait_ge(w1_split, k // FC + 1)
                if u == 0:
                    pe.wait_ge(p1T_ready, B * T - 1)
                if u >= 2:
                    pe.wait_ge(gelu_done, u - 1)
                cols = slice(S * half, S * half + S)
                three_passes((6 + u % 2,), w1h[:, k // FC, k % FC, :], w1l[:, k // FC, k % FC, :], xh[:, cols],
                             xl[:, cols], True, True).then_inc(mm1_done, 1)

            def half_product2(u):
                half, k = u // PAIR, u % PAIR
                if k % FC == 0:
                    pe.wait_ge(w2_split, k // FC + 1)
                pe.wait_ge(lo_done, u + 1)
                three_passes((2 * (k // FC) + half,), w2h[:, k // FC, k % FC, :], w2l[:, k // FC, k % FC, :],
                             hh_half[:, u % 8, :], hl_half[:, u % 8, :], k % FC == 0,
                             k % FC == FC - 1).then_inc(mm2_done, 1)

            attend1(B * T - 1)
            for u in range(2 * PAIR):
                half_product1(u)
                if u == ROUTER0:
                    router(0)
                if u == TURN1:
                    pe.wait_ge(xn_ready, B + 2)
                    turn_x(xn, 1)
                if u == ROUTER1:
                    router(1)
                if u >= LAG:
                    half_product2(u - LAG)

            def product2(k, e, u):
                slot = k // FC
                if k % FC == 0:
                    pe.wait_ge(w2_split, e + 1)
                    pe.wait_ge(y_used, e * 2 - 2)
                pe.wait_ge(lo_done, u + 1)
                three_passes((2 * slot, 2 * slot + 1), w2h[:, slot, k % FC, :], w2l[:, slot, k % FC, :],
                             hh[:, k % 4, :], hl[:, k % 4, :], k % FC == 0, k % FC == FC - 1).then_inc(mm2_done, 1)

            def pair(it, first):
                for k in range(PAIR):
                    u, slot = it * PAIR + k, k // FC
                    if k % FC == 0:
                        pe.wait_ge(w1_split, it * 2 + (slot - 1))
                    if first and k == 0:
                        pe.wait_ge(gelu_done, u)
                    elif first and k == 1:
                        pe.wait_ge(combineT_ready, B)
                    else:
                        pe.wait_ge(gelu_done, u - 1)
                    three_passes((6 - 2 * (k % 2), 7 - 2 * (k % 2)), w1h[:, slot, k % FC, :], w1l[:, slot, k % FC, :],
                                 xh[:, :], xl[:, :], True, True).then_inc(mm1_done, 1)
                    if first and k == 0:
                        turn_combine()
                    if k >= LAG:
                        product2(k - LAG, it * 2 + ((k - LAG) // FC - 2), u - LAG)
                    elif first:
                        half_product2(u - LAG)
                    else:
                        product2(PAIR + k - LAG, None, u - LAG)

            pair(2, True)
            with pe.Fori(3, E // 2 + 1) as it:
                pair(it, False)
            product2(PAIR - 2, E - 1, E // 2 * PAIR + PAIR - 2)
            pe.wait_ge(y_used, B * (E - 1))
            for b in range(B):
                pe.wait_ge(sum_ready, B * (E - 2) + b + 1)
                for t in range(T):
                    cols = slice(S * b + P * t, S * b + P * t + P)
                    mm(bank(b)[:, D * t:D * t + D], acc[:, cols], ident, start=(t == 0), stop=False)
            k = PAIR - 1
            pe.wait_ge(lo_done, E // 2 * PAIR + k + 1)
            for half in range(2):
                cols = slice(S * half, S * half + S)
                three_passes((2 + half,), w2h[:, 1, k % FC, :], w2l[:, 1, k % FC, :], hh[:, k % 4, cols],
                             hl[:, k % 4, cols], False, True).then_inc(last_y, 1)
            for b in range(B):
                pe.wait_ge(y_used, B * (E - 1) + b + 1)
                for t in range(T):
                    last = mm(bank(b)[:, D * t:D * t + D], part[:, b, P * t:P * t + P], ident, start=False)
                last.then_inc(y_turned, 1)

        @block.vector
        def _(dve):
            v = nc.vector
            steps = [0]

            def done(ins):
                steps[0] += 1
                ins.then_inc(dve_step, 1)
                dve.wait_ge(dve_step, steps[0])

            def take_moments(b):
                for t in range(T):
                    last = v.bn_stats(stats[:, b, t, :], x[:, b, t, :])
                done(last)
                for t in range(T):
                    last = v.bn_aggr(moments[:, b, t, :], stats[:, b, t, :])
                last.then_inc(moments_ready, 1)

            def normalize(n, b):
                dve.wait_ge(rstd_ready, B * n + b + 1)
                for t in range(T):
                    last = v.tensor_scalar(xn[:, b, t, :], x[:, b, t, :], moments[:, b, t, 0:1], rstd[:, b, t:t + 1],
                                           ALU.subtract, ALU.mult)
                last.then_inc(xn_ready, 1)

            def wide(a, n):
                return a.unsqueeze(len(a.shape)).to_broadcast([*a.shape, n])

            def flat(a):
                return a.rearrange("p i d -> p (i d)")

            v.memset(xn[:, 0], 0.0).then_inc(zeros_ready, 1)
            v.memset(k1_band[:, :, :, :], 0.0)
            v.memset(v1_band, 0.0).then_inc(band_zero, 1)
            dve.wait_ge(setup0_in, 16)
            for b in range(B):
                last = v.tensor_copy(ctx_rep[:, b], ctxT[0:C + 1, J * b:J * b + J].unsqueeze(1).to_broadcast([C + 1, T, J]))
            last.then_inc(ctx_rep_ready, 1)
            dve.wait_ge(wq0T_psum, 1)
            v.tensor_copy(wq0T[:, :], bank(7)[:, 0:D])
            dve.wait_ge(kv0_psum, 1)
            v.tensor_copy(k0T[:, :, :].rearrange("d b j -> d (b j)"), bank(6)[:, 0:B * J]).then_inc(k0_ready, 1)
            dve.wait_ge(x_in[0], 16)
            take_moments(0)
            dve.wait_ge(key0_psum, 1)
            v.tensor_copy(key0[:, :, :].rearrange("d b j -> d (b j)"), bank(5)[:, 0:B * J])
            v.tensor_copy(bias0[:, :, :].rearrange("p b j -> p (b j)"), bank(5)[:, B * J:2 * B * J]).then_inc(key0_ready, 1)
            dve.wait_ge(x_in[1], 16)
            take_moments(1)
            dve.wait_ge(key0_ready, 1)
            for b in range(B):
                s = bank(2 + b)[:, 0:P].rearrange("p (i j) -> p i j", j=J)
                dve.wait_ge(s0_psum, b + 1)
                dve.wait_ge(rstd_ready, b + 1)
                for t in range(T):
                    last = v.scalar_tensor_tensor(out=raw0[:, b, t, :], in0=s[:, t, :], scalar=rstd[:, b, t:t + 1],
                                                  in1=bias0[:, b, :], op0=ALU.mult, op1=ALU.add)
                done(last)
                done(v.tensor_reduce(small0[:, 0, b, :], raw0[:, b], X, ALU.max))
                v.tensor_tensor(shifted0[:, b], raw0[:, b], wide(small0[:, 0, b, :], J), ALU.subtract).then_inc(sh0_ready, 1)
            dve.wait_ge(kv0_psum, 2)
            dve.wait_ge(setup1_in, 16)
            for b in range(B):
                dve.wait_ge(e0_ready, b + 1)
                done(v.tensor_reduce(small0[:, 1, b, :], shifted0[:, b], X, ALU.add))
                done(v.reciprocal(small0[:, 2, b, :], small0[:, 1, b, :]))
                v.tensor_tensor(probs0[:, b], shifted0[:, b], wide(small0[:, 2, b, :], J), ALU.mult).then_inc(p0_ready, 1)
                v.tensor_tensor(v0_band[:, b], bank(4)[:, P * b:P * b + P].unsqueeze(1).to_broadcast([P, T, D]),
                                wide(bandmask, D), ALU.mult).then_inc(v0_ready, 1)
            v.tensor_scalar(c0x2[:, :], in_c, 2.0, None, ALU.mult).then_inc(c0x2_ready, 1)
            done(v.tensor_copy(wgT[:, 0, :], wgT_in))
            v.tensor_tensor(wgT[:, 1, :], wgT_in, wgT[:, 0, :].bitcast(F32), ALU.subtract)
            for b in range(B):
                dve.wait_ge(o0_psum, b + 1)
                done(v.tensor_tensor(flat(x[:, b]), bank(b), flat(x[:, b]), ALU.add))
                take_moments(b)
            dve.wait_ge(const_psum, 1)
            done(v.tensor_tensor(bias_t0[:, :], bank(2)[:, 0:3], bias_f[:, 0:3], ALU.add))
            normalize(1, 0)
            normalize(1, 1)
            v.tensor_scalar(bias_t0[:, 0:2], bias_t0[:, 0:2], 0.5, None, ALU.mult)
            v.tensor_scalar(bias_t1[:, 0:2], bias_f[:, 0:2], 0.5, None, ALU.mult)
            v.tensor_copy(bias_t1[:, 2:3], bias_f[:, 2:3]).then_inc(bias_ready, 1)
            dve.wait_ge(kv1_psum, 2)
            dve.wait_ge(band_zero, 1)
            for h in range(2):
                rows = slice(DH * h, DH * h + DH)
                last = v.tensor_scalar(k1_band[rows, :, h, :], bank(5)[rows, :].rearrange("p (c n) -> p c n", c=HC),
                                       DH ** -0.5, None, ALU.mult)
            last.then_inc(k1_ready, 1)
            dve.wait_ge(gates_ready, 1)
            v.tensor_scalar(keep_c, gates[:, 0, 0, :], 1.0, in_c, ALU.add, ALU.mult)
            dve.wait_ge(gates_ready, 3)
            done(v.scalar_tensor_tensor(out=new_c, in0=gates[:, 0, 1, :], scalar=1.0, in1=gates[:, 0, 2, :],
                                        op0=ALU.add, op1=ALU.mult))
            v.tensor_tensor(c1x2, keep_c, new_c, ALU.add).then_inc(c_ready, 1)
            dve.wait_ge(c_ready, 1)
            dve.wait_ge(gates_ready, 4)
            v.scalar_tensor_tensor(out=keep_c, in0=gates[:, 1, 0, :], scalar=1.0, in1=c1x2, op0=ALU.add, op1=ALU.mult)
            dve.wait_ge(gates_ready, 6)
            done(v.scalar_tensor_tensor(out=new_c, in0=gates[:, 1, 1, :], scalar=1.0, in1=gates[:, 1, 2, :],
                                        op0=ALU.add, op1=ALU.mult))
            v.scalar_tensor_tensor(out=c2x2, in0=keep_c, scalar=0.5, in1=new_c, op0=ALU.mult,
                                   op1=ALU.add).then_inc(c_ready, 1)
            for b in range(B):
                dve.wait_ge(h_psum, b + 1)
                v.tensor_tensor(flat(x[:, b]), bank(6 + b), flat(x[:, b]), ALU.add).then_inc(x2_ready, 1)
                dve.wait_ge(x2_ready, b + 1)
                take_moments(b)

            def max1(t):
                dve.wait_ge(s1_psum, t + 1)
                v.tensor_reduce(small1[:, 0, t % 3, :], bank(2 + t % 3).rearrange("p (h j) -> p h j", j=J), X,
                                ALU.max).then_inc(max1_done, 1)

            def shift1(t):
                dve.wait_ge(max1_done, t + 1)
                if t >= 3:
                    dve.wait_ge(p1_ready, t - 2)
                v.tensor_tensor(shifted1[:, t % 3], bank(2 + t % 3).rearrange("p (h j) -> p h j", j=J),
                                wide(small1[:, 0, t % 3, :], J), ALU.subtract).then_inc(sh1_ready, 1)

            def sum1(t):
                dve.wait_ge(e1_ready, t + 1)
                v.tensor_reduce(small1[:, 1, t % 3, :], shifted1[:, t % 3], X, ALU.add).then_inc(sum1_done, 1)

            def reciprocal1(t):
                dve.wait_ge(sum1_done, t + 1)
                v.reciprocal(small1[:, 2, t % 3, :], small1[:, 1, t % 3, :]).then_inc(r1_ready, 1)

            def attended(b):
                dve.wait_ge(o1_step, T * (b + 1))
                dve.wait_ge(x2b_ready, b + 1)
                done(v.tensor_tensor(flat(x[:, b]), bank(7 if b == 0 else 1), flat(x[:, b]), ALU.add))
                take_moments(b)

            def x_lo(b):
                dve.wait_ge(xT_ready, 2 * B + b + 1)
                v.tensor_tensor(xl[:, S * b:S * b + S], bank(b), xh[:, S * b:S * b + S].bitcast(F32),
                                ALU.subtract).then_inc(xl_ready, 1)

            for t in range(2):
                max1(t)
                shift1(t)
            for t in range(B * T):
                if t + 2 < B * T:
                    max1(t + 2)
                sum1(t)
                if t + 2 < B * T:
                    shift1(t + 2)
                reciprocal1(t)
                if t == 5:
                    attended(0)
                if t == 6:
                    normalize(3, 0)
            x_lo(0)

            gs, gp, eq, first, rest, com = (a[:, :, :] for a in (g_shift, g_prob, g_eq, g_first, g_rest, combine))
            small = [g_small[:, n] for n in range(4)]
            down = descend.unsqueeze(1).to_broadcast([P, B * T, E])

            def router_shift(b):
                s = bank(3)[:, E * T * b:E * T * (b + 1)].rearrange("p (t e) -> p t e", e=E)
                top = g_small[:, 0, T * b:T * b + T]
                dve.wait_ge(logit_psum, b + 1)
                done(v.tensor_reduce(top, s, X, ALU.max))
                v.tensor_tensor(g_shift[:, T * b:T * b + T, :], s, wide(top, E), ALU.subtract).then_inc(gexp_arg, 1)

            def first_of(chosen):
                done(v.tensor_reduce(small[3], eq, X, ALU.max))
                done(v.tensor_tensor(chosen, eq, wide(small[3], E), ALU.is_equal))

            def pick_first():
                dve.wait_ge(gexp_arg, B)
                done(v.scalar_tensor_tensor(out=eq, in0=gs, scalar=0.0, in1=down, op0=ALU.is_equal, op1=ALU.mult))
                first_of(first)

            def pick_second():
                done(v.scalar_tensor_tensor(out=rest, in0=first, scalar=LOWEST, in1=gs, op0=ALU.mult, op1=ALU.add))
                done(v.tensor_reduce(small[2], rest, X, ALU.max))
                done(v.tensor_tensor(eq, rest, wide(small[2], E), ALU.is_equal))

            def both_picks():
                done(v.tensor_tensor(eq, eq, down, ALU.mult))
                first_of(com)
                done(v.tensor_tensor(eq, com, first, ALU.add))

            def router_weights():
                dve.wait_ge(gexp_ready, B)
                done(v.tensor_reduce(small[1], gp, X, ALU.add))
                done(v.reciprocal(small[2], small[1]))
                done(v.tensor_tensor(gp, gp, wide(small[2], E), ALU.mult))
                v.tensor_tensor(com, eq, gp, ALU.mult).then_inc(combine_ready, 1)

            def weigh(half, slot, e, last=False):
                cols = slice(S * half, S * half + S)
                static = isinstance(e, int)
                if last:
                    dve.wait_ge(last_y, half + 1)
                else:
                    dve.wait_ge(mm2_done, e * FC + 3 * FC)
                for n in range(1, 2 if static and e == 1 else 3):
                    dve.wait_ge(cwb_in[n], 16)
                dve.wait_ge(sum_ready, e * 2 + (half - 1))
                w = cwb[:, e, cols] if static else cwb[:, bass.ds(e, 1), cols].rearrange("p e n -> p (e n)")
                v.scalar_tensor_tensor(out=part[:, half], in0=bank(2 * slot + half), scalar=b2T[:, bass.ds(e, 1)],
                                       in1=w, op0=ALU.add, op1=ALU.mult).then_inc(y_used, 1)
                if not last:
                    dve.wait_ge(y_used, e * 2 + (half + 1))
                    v.tensor_tensor(acc[:, cols], acc[:, cols], part[:, half], ALU.add).then_inc(sum_ready, 1)

            attended(1)
            for u in range(2 * PAIR):
                dve.wait_ge(hi_done, u + 1)
                if u >= 8:
                    dve.wait_ge(mm2_done, u - 7)
                v.tensor_tensor(hl_half[:, u % 8, :], hid_half[:, u % 4, :], hh_half[:, u % 8, :].bitcast(F32),
                                ALU.subtract).then_inc(lo_done, 1)
                if u == 0:
                    normalize(3, 1)
                if u == X_LO1:
                    x_lo(1)
                if u == SHIFT0:
                    router_shift(0)
                if u == SHIFT1:
                    router_shift(1)
                if u == SHIFT1 + 1:
                    pick_first()
                if u == SHIFT1 + 2:
                    pick_second()
                if u == SHIFT1 + 3:
                    both_picks()
                if u == 12:
                    router_weights()
                if u in (13, 14):
                    half = u - 13
                    dve.wait_ge(mm2_done, PAIR * half + FC)
                    v.tensor_copy(acc[:, S * half:S * half + S], bank(half)).then_inc(y_used, 1)
                if u == 15:
                    for b in range(B):
                        dve.wait_ge(combineT_psum, b + 1)
                        v.tensor_copy(combineT[:, S * b:S * b + S], bank(4 + b)[0:E, :]).then_inc(combineT_ready, 1)

            def pair(it, first):
                for k in range(PAIR):
                    u = it * PAIR + k
                    dve.wait_ge(hi_done, u + 1)
                    dve.wait_ge(mm2_done, u - 3)
                    v.tensor_tensor(hl[:, k % 4, :], hid[:, k % 2, :], hh[:, k % 4, :].bitcast(F32),
                                    ALU.subtract).then_inc(lo_done, 1)
                    if first and k == 2:
                        dve.wait_ge(cwb_in[0], 16)
                        dve.wait_ge(y_used, B)
                        for half in range(2):
                            cols = slice(S * half, S * half + S)
                            v.scalar_tensor_tensor(out=acc[:, cols], in0=acc[:, cols], scalar=b2T[:, 0:1],
                                                   in1=cwb[:, 0, cols], op0=ALU.add,
                                                   op1=ALU.mult).then_inc(sum_ready, 1)
                    if k in ((3, 4) if first else (1, 2)):
                        weigh((k + 1) % 2 if not first else k - 3, 1, it * 2 - 3)
                    if k in (5, 6):
                        weigh(k - 5, 0, it * 2 - 2)

            pair(2, True)
            with dve.Fori(3, E // 2 + 1) as it:
                pair(it, False)
            for half in range(2):
                weigh(half, 1, E - 1, last=True)
            for b in range(B):
                dve.wait_ge(y_turned, b + 1)
                v.tensor_tensor(flat(x[:, b]), bank(b), flat(x[:, b]), ALU.add).then_inc(res_ready, 1)


NAMES = ["x", "xT", "setup0", "setup1", "gate_T", "wq1", "wk1", "wv1", "wo1", "bo1", "w1", "w2"]


def lay_out(a):
    import numpy as np

    def rows(parts, pack):
        out = np.zeros((P, sum(n for _, n in pack)), np.float32)
        at = 0
        for name, n in pack:
            p = parts[name]
            out[:p.shape[0], at:at + n] = p
            at += n
        return out

    one = np.ones((1, B * J), np.float32)
    ident = np.eye(P, dtype=np.float32)
    p = np.arange(P)[:, None]
    setup0 = {
        "ctxT": np.concatenate([a["ctx_768"].reshape(B * J, C).T, one]),
        "wq0": a["L0_xattn_Wq"],
        "wk0": np.concatenate([a["L0_xattn_Wk"], a["L0_xattn_bk"][None]]),
        "wv0": np.concatenate([a["L0_xattn_Wv"], a["L0_xattn_bv"][None]]),
        "centre": ident - np.float32(1 / D),
        "bq0": a["L0_xattn_bq"][:, None],
    }
    setup1 = {
        "ident": ident,
        "bandmask": (p // J == np.arange(T)).astype(np.float32),
        "descend": np.tile(np.arange(E, 0, -1, dtype=np.float32), (P, 1)),
        "minus_half": np.full((P, T), -0.5, np.float32),
        "euler": np.full((P, T * E), np.e, np.float32),
        "bias_f": np.stack([a["L0_ffn_" + n] for n in ("bf", "bi", "bc", "bo")], axis=1),
        "in_c": a["L0_ffn_in_c"][:, None],
        "wgT": a["L1_ffn_w_gate"].T,
        "b2T": a["L1_ffn_b2"].T,
        "b1": a["L1_ffn_b1"].reshape(E, FC, P).transpose(2, 0, 1).reshape(P, E * FC),
    }
    return {
        "x": a["x"],
        "xT": a["x"].reshape(B, P, T, D).transpose(3, 0, 2, 1).reshape(D, B, S),
        "setup0": rows(setup0, PACK0),
        "setup1": rows(setup1, PACK1),
        "gate_T": np.stack([a["L0_ffn_" + n].T for n in ("wf", "wi", "wc", "wo", "uf", "ui", "uc", "uo")], axis=1),
        "wq1": a["L1_xattn_w_q"].reshape(D, HC, P),
        "wk1": a["L1_xattn_w_k"].reshape(C, HC, P),
        "wv1": a["L1_xattn_w_v"].reshape(C, HC, P),
        "wo1": a["L1_xattn_w_o"].reshape(HC, P, D).transpose(1, 0, 2),
        "bo1": a["L1_xattn_b_o"],
        "w1": a["L1_ffn_W1"].reshape(E, D, FC, P).transpose(1, 0, 2, 3),
        "w2": a["L1_ffn_W2"].reshape(E, FC, P, D).transpose(2, 0, 1, 3),
    }


def kernel(**inputs):
    import numpy as np
    import concourse.bacc as bacc
    from concourse.bass_utils import run_bass_kernel_spmd

    laid = lay_out({n: np.asarray(x) for n, x in inputs.items()})
    nc = bacc.Bacc("TRN2", target_bir_lowering=False, num_devices=1)
    arrays, views = {}, {}
    for name in NAMES:
        a = np.ascontiguousarray(laid[name])
        arrays[f"in_{name}"] = a
        views[name] = nc.dram_tensor(f"in_{name}", a.shape, mybir.dt.from_np(a.dtype), kind="ExternalInput").ap()
    out = nc.dram_tensor("out_x", (B, S, D), F32, kind="ExternalOutput").ap()
    two_layers(nc, views, out)
    r = run_bass_kernel_spmd(nc, [arrays], core_ids=[0])
    return r.results[0]["out_x"]
```

```python
from contextlib import ExitStack

import concourse.bass as bass
from concourse import mybir

F32 = mybir.dt.float32
F32R = mybir.dt.float32r
ALU = mybir.AluOpType
ACT = mybir.ActivationFunctionType
X = mybir.AxisListType.X

P = 128
B = 2
S = 512
T = S // P
D = 128
C = 96
J = 32
H = 16
DH = 64
HC = H * DH // P
KC = H * J // P
HPC = P // J
E = 8
F = 512
FC = F // P
LAG = 2
PAIR = 2 * FC
EPS = 1e-5
ATTEND_LATE = 7
PIECES = [(b, slice(n, n + T // 2), bank) for b, n, bank in ((0, 0, 0), (0, T // 2, 1), (1, 0, 6), (1, T // 2, 7))]
SCORE_BANKS = (2, 3, 4, 0)
LOWEST = -3e38
WARM_UP, WARM_KEYS, WARM_COPY, WARM_SCORES = 6, 3, 3, 0

PACK0 = [("ctxT", B * J), ("wq0", D), ("wk0", D), ("wv0", D), ("centre", D), ("bq0", 1)]
PACK1 = [("ident", P), ("bandmask", T), ("descend", E), ("minus_half", T), ("euler", T * E), ("bias_f", 4),
         ("in_c", 1), ("wgT", E), ("b1", E * FC), ("b2T", E)]

ROUTER0, TURN1, ROUTER1 = 1, 4, 6
XH1 = 4
SHIFT0, X_LO1, SHIFT1, WEIGHTS = 2, 4, 6, 12


def two_layers(nc, i, out):
    ctx = ExitStack()
    with ctx:
        def sb(name, shape, dt=F32):
            return ctx.enter_context(nc.sbuf_tensor(name, shape, dt))

        def sem(name):
            return ctx.enter_context(nc.semaphore(name))

        psum = ctx.enter_context(nc.psum_tensor("psum", [P, 8, 512], F32))

        def bank(n):
            return psum[:, n, :]

        def overlay(name, shapes, whole):
            words = whole[1]
            for d in whole[2:]:
                words *= d
            space, at, views = sb(name, [P, words]), 0, []
            for shape in [whole, *shapes]:
                n = 1
                for d in shape[1:]:
                    n *= d
                start = 0 if shape is whole else at
                at = at if shape is whole else at + n
                assert at <= words
                names = " ".join("abcd"[:len(shape) - 1])
                sizes = dict(zip("bcd", shape[2:]))
                views.append(space[0:shape[0], start:start + n].rearrange(f"p ({names}) -> p {names}", **sizes))
            return views

        def packed(name, parts):
            space, at, views = sb(name, [P, sum(n for _, n in parts)]), 0, {}
            for part, n in parts:
                views[part] = space[:, at:at + n]
                at += n
            return space, views

        x = sb("x", [P, B, T, D])
        xn = sb("xn", [P, B, T, D])
        xT = sb("xT", [D, B, S])
        stats = sb("stats", [P, B, T, 6])
        moments = sb("moments", [P, B, T, 2])
        var_eps = sb("var_eps", [P, B, T])
        rstd = sb("rstd", [P, B, T])

        setup0, v0 = packed("setup0", PACK0)
        ctxT, wq0, wk0, wv0 = (v0[n] for n in ("ctxT", "wq0", "wk0", "wv0"))
        centre, bq0 = v0["centre"], v0["bq0"]
        setup1, v1 = packed("setup1", PACK1)
        ident, bandmask, descend = v1["ident"], v1["bandmask"], v1["descend"]
        minus_half, euler, bias_f, in_c = v1["minus_half"], v1["euler"], v1["bias_f"], v1["in_c"]
        wgT_in, b2T, b1 = v1["wgT"], v1["b2T"], v1["b1"].rearrange("p (e c) -> p e c", c=FC)

        zeros = sb("zeros", [P, P])
        ctx_rep = sb("ctx_rep", [C + 1, B, T, J])
        wq0T = sb("wq0T", [D, D])
        bq0_wide = sb("bq0_wide", [D, P])
        k0T = sb("k0T", [D, B, J])
        v0_band = sb("v0_band", [P, B, T, D])
        key0 = sb("key0", [D, B, J])
        bias0 = sb("bias0", [P, B, J])

        gate_T = sb("gate_T", [D, 8, D])
        gate_uT = sb("gate_uT", [D, 4, D])
        bias_t0 = sb("bias_t0", [D, 3])
        bias_t1 = sb("bias_t1", [D, 3])

        wq1T = sb("wq1T", [P, HC, D])
        k1_band = sb("k1_band", [P, HC, 2, B * J])
        bo1 = sb("bo1", [P, D])
        key1 = sb("key1", [D, B, H, J])
        val1 = sb("val1", [P, B, KC, D])

        raw0 = sb("raw0", [P, B, T, J])
        shifted0 = sb("shifted0", [P, B, T, J])
        probs0 = sb("probs0", [P, B, T, J])
        probs0T = sb("probs0T", [P, B, P])
        small0 = sb("small0", [P, 3, B, T])
        shifted1 = sb("shifted1", [P, 3, H, J])
        probs1 = sb("probs1", [P, 2, H, J])
        probs1T = sb("probs1T", [P, 2, KC, P])
        small1 = sb("small1", [P, 3, 3, H])

        table_in = sb("table_in", [P, 1])
        wgT = sb("wgT", [D, 2, E], F32R)
        xh = sb("xh", [D, B * S], F32R)
        xl = sb("xl", [D, B * S], F32R)
        g_shift = sb("g_shift", [P, B * T, E])
        g_prob = sb("g_prob", [P, B * T, E])
        g_small = sb("g_small", [P, 4, B * T])
        g_eq = sb("g_eq", [P, B * T, E])
        g_first = sb("g_first", [P, B * T, E])
        g_rest = sb("g_rest", [P, B * T, E])
        combine = sb("combine", [P, B * T, E])
        combineT = sb("combineT", [E, B * S])
        cwb, gates, keep_c, new_c, c1x2, c2x2, hT, v1_band = overlay("cwb", [
            [D, 2, 3, S], [D, S], [D, S], [D, S], [D, S], [D, B, S], [P, HC, B, HPC, J]], [P, E, B * S])
        hid, wk1, wv1 = overlay("hid", [[C, HC, P], [C, HC, P]], [P, 2, B * S])
        part, wo1 = overlay("part", [[P, HC, D]], [P, 2, S])
        acc, wq1 = overlay("acc", [[D, HC, P]], [D, B * S])
        combine_dram = nc.dram_tensor("combine_dram", [E, B * S], F32, kind="Internal").ap()

        w1 = sb("w1", [D, E, FC, P])
        w2 = sb("w2", [P, E, FC, D])
        w1h = sb("w1h", [D, 2, FC, P], F32R)
        w1l = sb("w1l", [D, 2, FC, P], F32R)
        w2h = sb("w2h", [P, 2, FC, D], F32R)
        w2l = sb("w2l", [P, 2, FC, D], F32R)
        hh = sb("hh", [P, 4, B * S], F32R)
        hl = sb("hl", [P, 4, B * S], F32R)
        hid_half = hid.rearrange("p a (b n) -> p (a b) n", b=B)
        hh_half = hh[:, :, :].rearrange("p a (b n) -> p (a b) n", b=B)
        hl_half = hl[:, :, :].rearrange("p a (b n) -> p (a b) n", b=B)

        x_in, xT_in, w1_in, w2_in = ([sem(f"{a}_in{n}") for n in range(2)] for a in ("x", "xT", "w1", "w2"))
        cwb_in = [sem(f"cwb_in{n}") for n in range(3)]
        (setup0_in, setup1_in, gate_in, wq1_in, wk1_in, wv1_in, wo1_in, bo1_in, combine_out, out_done) = (
            sem(n) for n in ("setup0_in", "setup1_in", "gate_in", "wq1_in", "wk1_in", "wv1_in", "wo1_in", "bo1_in",
                             "combine_out", "out_done"))
        zeros_ready = sem("zeros_ready")
        dve_step, pool_step = sem("dve_step"), sem("pool_step")
        bq_wide_ready, ctx_rep_ready, gate_uT_ready = sem("bq_wide_ready"), sem("ctx_rep_ready"), sem("gate_uT_ready")
        wq0T_psum = sem("wq0T_psum")
        const_psum, bias_ready = sem("const_psum"), sem("bias_ready")
        kv0_psum, k0_ready, v0_ready = sem("kv0_psum"), sem("k0_ready"), sem("v0_ready")
        key0_psum, key0_ready = sem("key0_psum"), sem("key0_ready")
        wq1T_psum, wq1T_ready, band_zero = sem("wq1T_psum"), sem("wq1T_ready"), sem("band_zero")
        kv1_psum, k1_ready, v1_ready = sem("kv1_psum"), sem("k1_ready"), sem("v1_ready")
        key1_psum, key1_ready = sem("key1_psum"), sem("key1_ready")
        val1_psum, val1_ready = sem("val1_psum"), sem("val1_ready")
        moments_ready, rstd_ready, xn_ready = sem("moments_ready"), sem("rstd_ready"), sem("xn_ready")
        xT_psum, xT_ready = sem("xT_psum"), sem("xT_ready")
        s0_psum, sh0_ready, e0_ready, p0_ready = sem("s0_psum"), sem("sh0_ready"), sem("e0_ready"), sem("p0_ready")
        p0T_psum, p0T_ready, o0_psum = sem("p0T_psum"), sem("p0T_ready"), sem("o0_psum")
        added0 = sem("added0")
        z_psum, gates_ready, c_ready = sem("z_psum"), sem("gates_ready"), sem("c_ready")
        ho_psum, hT_ready, h_psum = sem("ho_psum"), sem("hT_ready"), sem("h_psum")
        x2_ready, x2b_ready = sem("x2_ready"), sem("x2b_ready")
        s1_psum, max1_done, sh1_ready, e1_ready = sem("s1_psum"), sem("max1_done"), sem("sh1_ready"), sem("e1_ready")
        sum1_done, r1_ready, p1_ready = sem("sum1_done"), sem("r1_ready"), sem("p1_ready")
        added1, stats1_ready = sem("added1"), sem("stats1_ready")
        p1T_psum, p1T_ready, o1_step = sem("p1T_psum"), sem("p1T_ready"), sem("o1_step")
        xl_ready, logit_psum = sem("xl_ready"), sem("logit_psum")
        gexp_arg, gexp_ready = sem("gexp_arg"), sem("gexp_ready")
        combine_ready, combineT_psum, combineT_ready = sem("combine_ready"), sem("combineT_psum"), sem("combineT_ready")
        w1_split, w2_split = sem("w1_split"), sem("w2_split")
        mm1_done, mm2_done = sem("mm1_done"), sem("mm2_done")
        gelu_done, hi_done, lo_done = sem("gelu_done"), sem("hi_done"), sem("lo_done")
        last_y, y_used, sum_ready = sem("last_y"), sem("y_used"), sem("sum_ready")
        y_turned, res_ready = sem("y_turned"), sem("res_ready")

        x_v = i["x"].rearrange("b (p i) d -> b p i d", i=T)
        out_v = out.rearrange("b (p i) d -> b p i d", i=T)

        block = ctx.enter_context(nc.Block())

        @block.sync
        def _(sp):
            sp.dma_start(setup0[:, :], i["setup0"]).then_inc(setup0_in, 16)
            sp.dma_start(x[:, 0], x_v[0]).then_inc(x_in[0], 16)
            sp.dma_start(xT[:, 1], i["xT"][:, 1]).then_inc(xT_in[1], 16)
            sp.dma_start(wv1, i["wv1"]).then_inc(wv1_in, 16)
            sp.dma_start(wq1[:, :, :], i["wq1"]).then_inc(wq1_in, 16)
            sp.dma_start(gate_T[:, :, :], i["gate_T"]).then_inc(gate_in, 16)
            sp.dma_start(wo1[:, :, :], i["wo1"]).then_inc(wo1_in, 16)
            sp.dma_start(w1[:, 0:2], i["w1"][:, 0:2]).then_inc(w1_in[0], 16)
            sp.dma_start(w2[:, 0:2], i["w2"][:, 0:2]).then_inc(w2_in[0], 16)
            sp.dma_start(w1[:, 2:E], i["w1"][:, 2:E]).then_inc(w1_in[1], 16)
            sp.dma_start(w2[:, 2:E], i["w2"][:, 2:E]).then_inc(w2_in[1], 16)
            sp.wait_ge(combineT_ready, B)
            sp.dma_start(combine_dram, combineT[:, :]).then_inc(combine_out, 16)
            sp.wait_ge(combine_out, 16)
            for n, (e, m) in enumerate(((0, 1), (1, 1), (2, E - 2))):
                sp.dma_start(cwb[:, e:e + m, :], combine_dram[e:e + m, :].partition_broadcast(P)).then_inc(cwb_in[n], 16)
            for n, (b, tiles, _) in enumerate(PIECES):
                sp.wait_ge(res_ready, n + 1)
                sp.dma_start(out_v[b, :, tiles], x[:, b, tiles]).then_inc(out_done, 16)
            sp.wait_ge(out_done, 16 * len(PIECES))

        @block.gpsimd
        def _(pool):
            steps = [0]

            def done(ins):
                steps[0] += 1
                ins.then_inc(pool_step, 1)
                pool.wait_ge(pool_step, steps[0])

            def split(w, hi, lo, landed):
                pool.wait_ge(landed, 16)
                pool.tensor_copy(hi, w)
                pool.drain()
                return pool.tensor_tensor(lo, w, hi.bitcast(F32), ALU.subtract)

            def power(n, b):
                pool.wait_ge(moments_ready, B * n + b + 1)
                done(pool.tensor_scalar(var_eps[:, b, :], moments[:, b, :, 1], EPS, None, ALU.add))
                pool.tensor_tensor(rstd[:, b, :], var_eps[:, b, :], minus_half, ALU.pow).then_inc(rstd_ready, 1)

            pool.wait_ge(setup0_in, 16)
            pool.tensor_scalar(bq0_wide[:, :], centre, 0.0, bq0, ALU.mult, ALU.add).then_inc(bq_wide_ready, 1)
            pool.wait_ge(setup1_in, 16)
            for b in range(B):
                power(0, b)
            for b in range(B):
                power(1, b)
            for e in range(2):
                split(w1[:, e], w1h[:, e], w1l[:, e], w1_in[0]).then_inc(w1_split, 1)
                split(w2[:, e], w2h[:, e], w2l[:, e], w2_in[0]).then_inc(w2_split, 1)
            for b in range(B):
                power(2, b)
            for t in range(B * T):
                if t == 6:
                    power(3, 0)
                pool.wait_ge(r1_ready, t + 1)
                if t >= 2:
                    pool.wait_ge(p1T_psum, t - 1)
                pool.tensor_tensor(probs1[:, t % 2], shifted1[:, t % 3],
                                   small1[:, 2, t % 3, :].unsqueeze(2).to_broadcast([P, H, J]),
                                   ALU.mult).then_inc(p1_ready, 1)
                if t in (0, 2):
                    b = t // 2
                    pool.wait_ge(bo1_in, 16)
                    pool.wait_ge(xT_psum, B + b + 1)
                    pool.tensor_tensor(x[:, b], x[:, b], bo1[:, :].unsqueeze(1).to_broadcast([P, T, D]),
                                       ALU.add).then_inc(x2b_ready, 1)
            power(3, 1)
            for b in range(B):
                pool.wait_ge(gexp_arg, b + 1)
                gs, gp = (a[:, T * b:T * b + T, :].rearrange("p t e -> p (t e)") for a in (g_shift, g_prob))
                pool.tensor_tensor(gp, euler, gs, ALU.pow).then_inc(gexp_ready, 1)
            with pool.Fori(2, E // 2 + 1) as it:
                for k in range(2):
                    e = it * 2 + (k - 2)
                    pool.wait_ge(mm1_done, it * PAIR + (k * FC - FC))
                    split(w1[:, bass.ds(e, 1), :, :].rearrange("d e c p -> d (e c) p"), w1h[:, k], w1l[:, k],
                          w1_in[1]).then_inc(w1_split, 1)
                    pool.wait_ge(mm2_done, it * PAIR + (k * FC - FC))
                    split(w2[:, bass.ds(e, 1), :, :].rearrange("p e c d -> p (e c) d"), w2h[:, k], w2l[:, k],
                          w2_in[1]).then_inc(w2_split, 1)

        @block.scalar
        def _(act):
            act.dma_start(xT[:, 0], i["xT"][:, 0]).then_inc(xT_in[0], 16)
            act.dma_start(setup1[:, :], i["setup1"]).then_inc(setup1_in, 16)
            act.dma_start(x[:, 1], x_v[1]).then_inc(x_in[1], 16)
            act.dma_start(wk1, i["wk1"]).then_inc(wk1_in, 16)
            act.dma_start(bo1[:, :], i["bo1"].partition_broadcast(P)).then_inc(bo1_in, 16)

            def copy(o, x):
                return nc.scalar.activation(o, x, ACT.Copy)

            def evacuate_xT(n, b):
                act.wait_ge(xT_psum, B * (n - 1) + b + 1)
                copy(xT[:, b, :], bank(b)).then_inc(xT_ready, 1)

            for b in range(B):
                act.wait_ge(sh0_ready, b + 1)
                nc.scalar.activation(shifted0[:, b], shifted0[:, b], ACT.Exp).then_inc(e0_ready, 1)

            def evacuate_probs0(b):
                act.wait_ge(p0T_psum, b + 1)
                copy(probs0T[:, b, :], bank(2 + b)[:, 0:P]).then_inc(p0T_ready, 1)

            def evacuate_wq1(n):
                act.wait_ge(wq1T_psum, n + 1)
                copy(wq1T[:, 4 * n:4 * n + 4, :], bank(6 + n)).then_inc(wq1T_ready, 1)

            evacuate_wq1(0)
            evacuate_probs0(0)
            evacuate_probs0(1)
            act.wait_ge(kv1_psum, 1)
            act.wait_ge(band_zero, 1)
            v_src = bank(7).rearrange("p (k c b j) -> p c b k j", c=2, b=B, j=J)
            v_dst = v1_band.rearrange("p (k c) b h j -> p c h b k j", c=2)
            for c in range(2):
                for h2 in range(2):
                    rows = slice(DH * h2, DH * h2 + DH)
                    for b in range(B):
                        last = copy(v_dst[rows, c, 2 * c + h2, b], v_src[rows, c, b])
            last.then_inc(v1_ready, 1)

            def evacuate_key1(n):
                act.wait_ge(key1_psum, n + 1)
                copy(key1[:, :, 8 * n:8 * n + 8, :].rearrange("d b h j -> d h b j"),
                     bank(2 + n).rearrange("d (h b j) -> d h b j", b=B, j=J)).then_inc(key1_ready, 1)

            def evacuate_val1(b):
                act.wait_ge(val1_psum, b + 1)
                copy(val1[:, b, :, :], bank(4 + b)).then_inc(val1_ready, 1)

            act.wait_ge(gate_in, 16)
            nc.scalar.activation(gate_uT[:, :, :], gate_T[:, 4:8, :], ACT.Copy, scale=0.5).then_inc(gate_uT_ready, 1)
            evacuate_key1(0)
            evacuate_wq1(1)
            evacuate_key1(1)
            evacuate_xT(1, 0)
            evacuate_val1(0)
            act.wait_ge(bias_ready, 1)

            def gate(t, n):
                act.wait_ge(z_psum, 3 * t + n + 1)
                nc.scalar.activation(gates[:, t, n, :], bank(2 + 3 * t + n), ACT.Tanh,
                                     bias=(bias_t0, bias_t1)[t][:, n:n + 1],
                                     scale=0.5 if n < 2 else 1.0).then_inc(gates_ready, 1)

            gate(0, 0)
            gate(0, 1)
            evacuate_xT(1, 1)
            gate(0, 2)
            for n in range(3):
                gate(1, n)
            for b in range(B):
                act.wait_ge(ho_psum, b + 1)
                nc.scalar.activation(hT[:, b, :], bank(b), ACT.Tanh, bias=bias_f[:, 3:4]).then_inc(hT_ready, 1)
            evacuate_xT(2, 0)
            evacuate_val1(1)
            evacuate_xT(2, 1)

            def exp1(t):
                act.wait_ge(sh1_ready, t + 1)
                act.wait_ge(rstd_ready, 2 * B + t // T + 1)
                nc.scalar.activation(shifted1[:, t % 3], shifted1[:, t % 3], ACT.Exp,
                                     scale=rstd[:, t // T, t % T:t % T + 1]).then_inc(e1_ready, 1)

            def evacuate_xh(b):
                act.wait_ge(xT_psum, 2 * B + b + 1)
                copy(xh[:, S * b:S * b + S], bank(b)).then_inc(xT_ready, 1)

            exp1(0)
            exp1(1)
            for t in range(B * T):
                if t + 2 < B * T:
                    exp1(t + 2)
                if t == 6:
                    nc.scalar.activation(table_in[:, :], b1[:, 0, 0:1], ACT.Gelu)
                if t == 7:
                    evacuate_xh(0)
                act.wait_ge(p1T_psum, t + 1)
                if t >= 2:
                    act.wait_ge(o1_step, t - 1)
                copy(probs1T[:, t % 2], bank(6 - t % 2)).then_inc(p1T_ready, 1)

            for u in range(2 * PAIR):
                k = u % PAIR
                act.wait_ge(mm1_done, u + 1)
                if u >= 4:
                    act.wait_ge(lo_done, u - 3)
                nc.scalar.activation(hid_half[:, u % 4, :], bank(6 + u % 2), ACT.Gelu,
                                     bias=b1[:, k // FC, k % FC:k % FC + 1]).then_inc(gelu_done, 1)
                act.wait_ge(gelu_done, u + 1)
                if u >= 8:
                    act.wait_ge(mm2_done, u - 7)
                copy(hh_half[:, u % 8, :], hid_half[:, u % 4, :]).then_inc(hi_done, 1)
                if u == XH1:
                    evacuate_xh(1)
            with act.Fori(2, E // 2 + 1) as it:
                for k in range(PAIR):
                    u = it * PAIR + k
                    act.wait_ge(mm1_done, u + 1)
                    act.wait_ge(lo_done, u - 1)
                    h_in = psum[:, 6 - 2 * (k % 2):8 - 2 * (k % 2), :].rearrange("p a n -> p (a n)")
                    nc.scalar.activation(hid[:, k % 2, :], h_in, ACT.Gelu,
                                         bias=b1[:, bass.ds(it * 2 + (k // FC - 2), 1), k % FC]).then_inc(gelu_done, 1)
                    act.wait_ge(gelu_done, u + 1)
                    act.wait_ge(mm2_done, u - 3)
                    copy(hh[:, k % 4, :], hid[:, k % 2, :]).then_inc(hi_done, 1)

        @block.tensor
        def _(pe):
            def mm(o, lhsT, rhs, start=True, stop=True):
                return nc.tensor.matmul(o, lhsT, rhs, start=start, stop=stop, skip_group_check=True)

            def turn(o, x, k=P):
                return nc.tensor.transpose(o, x, ident[0:k, 0:k])

            def turn_x(src, b):
                for t in range(T):
                    last = turn(bank(b)[:, P * t:P * t + P], src[:, b, t, :])
                last.then_inc(xT_psum, 1)

            def stay_busy(n):
                for _ in range(n):
                    mm(bank(0)[:, 0:P], zeros[:, :], zeros[:, :])

            pe.wait_ge(zeros_ready, 1)
            stay_busy(WARM_UP)
            pe.wait_ge(setup0_in, 16)
            mm(bank(7)[:, 0:D], wq0, centre).then_inc(wq0T_psum, 1)
            mm(bank(6)[:, 0:B * J], wk0[0:C + 1, :], ctxT[0:C + 1, :]).then_inc(kv0_psum, 1)
            pe.wait_ge(ctx_rep_ready, 1)
            for b in range(B):
                last = mm(bank(4)[:, P * b:P * b + P], ctx_rep[:, b, :, :].rearrange("c i j -> c (i j)"), wv0[0:C + 1, :])
            last.then_inc(kv0_psum, 1)
            stay_busy(WARM_KEYS)
            pe.wait_ge(k0_ready, 1)
            pe.wait_ge(bq_wide_ready, 1)
            k0 = k0T[:, :, :].rearrange("d b j -> d (b j)")
            mm(bank(5)[:, 0:B * J], wq0T[:, :], k0)
            mm(bank(5)[:, B * J:2 * B * J], bq0_wide[:, :], k0).then_inc(key0_psum, 1)
            stay_busy(WARM_COPY)
            pe.wait_ge(key0_ready, 1)
            for b in range(B):
                pe.wait_ge(xT_in[b], 16)
                for t in range(T):
                    last = mm(bank(2 + b)[:, J * t:J * t + J], xT[:, b, P * t:P * t + P], key0[:, b, :])
                last.then_inc(s0_psum, 1)

            def keys_values1(n, w, landed):
                pe.wait_ge(landed, 16)
                for c in range(HC):
                    last = mm(bank(n)[:, B * J * c:B * J * (c + 1)], w[:, c, :], ctxT[0:C, :])
                last.then_inc(kv1_psum, 1)

            def query_weights1(n):
                pe.wait_ge(wq1_in, 16)
                for c in range(4):
                    last = mm(bank(6 + n)[:, P * c:P * c + P], wq1[:, 4 * n + c, :], centre)
                last.then_inc(wq1T_psum, 1)

            def turn_probs0(b):
                pe.wait_ge(p0_ready, b + 1)
                turn(bank(2 + b)[:, 0:P], probs0[:, b].rearrange("p i j -> p (i j)")).then_inc(p0T_psum, 1)

            def attend0(b):
                pe.wait_ge(p0T_ready, b + 1)
                pe.wait_ge(v0_ready, b + 1)
                mm(bank(b), probs0T[:, b, :], v0_band[:, b].rearrange("p i d -> p (i d)")).then_inc(o0_psum, 1)

            def keys1(n):
                pe.wait_ge(k1_ready, 1)
                pe.wait_ge(wq1T_ready, n + 1)
                for c in range(4):
                    last = mm(bank(2 + n)[:, P * c:P * c + P], wq1T[:, 4 * n + c, :],
                              k1_band[:, 4 * n + c].rearrange("p h n -> p (h n)"))
                last.then_inc(key1_psum, 1)

            stay_busy(WARM_SCORES)
            keys_values1(7, wv1, wv1_in)
            query_weights1(0)
            keys_values1(5, wk1, wk1_in)
            turn_probs0(0)
            pe.wait_ge(setup1_in, 16)
            pe.wait_ge(gate_in, 16)
            for n in range(3):
                last = mm(bank(1)[:, n:n + 1], gate_T[:, 4 + n, :], in_c)
            last.then_inc(const_psum, 1)
            attend0(0)
            turn_probs0(1)
            pe.wait_ge(bias_ready, 1)
            attend0(1)
            keys1(0)

            def values1(b, chunks):
                for k in chunks:
                    for c in range(2):
                        last = mm(bank(4 + b)[:, D * k:D * k + D],
                                  v1_band[:, 2 * k + c, b].rearrange("p h j -> p (h j)"), wo1[:, 2 * k + c, :],
                                  start=(c == 0), stop=(c == 1))
                if k == KC - 1:
                    last.then_inc(val1_psum, 1)

            pe.wait_ge(v1_ready, 1)
            query_weights1(1)
            pe.wait_ge(wo1_in, 16)
            values1(0, range(0, 2))
            keys1(1)
            pe.wait_ge(xn_ready, 1)
            turn_x(xn, 0)
            values1(0, range(2, KC))
            pe.wait_ge(xT_ready, 1)
            for n in range(3):
                pe.wait_ge(key1_ready, min(n + 1, 2))
                if n == 2:
                    pe.wait_ge(val1_ready, 1)
                mm(bank(2 + n), gate_T[:, n, :], xT[:, 0, :]).then_inc(z_psum, 1)
                if n == 1:
                    pe.wait_ge(xn_ready, 2)
                    turn_x(xn, 1)
            pe.wait_ge(xT_ready, 2)
            for n in range(3):
                mm(bank(5 + n), gate_T[:, n, :], xT[:, 1, :], stop=False)
            pe.wait_ge(c_ready, 1)
            pe.wait_ge(gate_uT_ready, 1)
            for n in range(3):
                mm(bank(5 + n), gate_uT[:, n, :], c1x2, start=False).then_inc(z_psum, 1)
            for b in range(B):
                mm(bank(b), gate_T[:, 3, :], xT[:, b, :], stop=False)
            pe.wait_ge(gates_ready, 4)
            values1(1, range(0, 2))
            pe.wait_ge(c_ready, 2)
            for b in range(B):
                mm(bank(b), gate_uT[:, 3, :], c2x2, start=False).then_inc(ho_psum, 1)
            for b in range(B):
                pe.wait_ge(hT_ready, b + 1)
                for t in range(T):
                    last = turn(bank(6 + b)[:, D * t:D * t + D], hT[:, b, P * t:P * t + P])
                last.then_inc(h_psum, 1)
                if b == 0:
                    values1(1, range(2, KC))

            def scores1(t):
                b, n = t // T, t % T
                pe.wait_ge(xT_ready, B + b + 1)
                if t >= 4:
                    pe.wait_ge(sh1_ready, t - 3)
                mm(bank(SCORE_BANKS[t % 4]), xT[:, b, P * n:P * n + P],
                   key1[:, b].rearrange("d h j -> d (h j)")).then_inc(s1_psum, 1)

            def turn1(t):
                pe.wait_ge(p1_ready, t + 1)
                if t >= 2:
                    pe.wait_ge(p1T_ready, t - 1)
                for k in range(KC):
                    last = turn(bank(6 - t % 2)[:, P * k:P * k + P],
                                probs1[:, t % 2, HPC * k:HPC * k + HPC, :].rearrange("p h j -> p (h j)"))
                last.then_inc(p1T_psum, 1)

            def attend1(t):
                pe.wait_ge(p1T_ready, t + 1)
                if t >= 2:
                    pe.wait_ge(added1, t - 1)
                for k in range(KC):
                    last = mm(bank((7, 1)[t % 2])[:, 0:D], probs1T[:, t % 2, k, :], val1[:, t // T, k, :],
                              start=(k == 0), stop=(k == KC - 1))
                last.then_inc(o1_step, 1)

            pe.wait_ge(x2_ready, 1)
            turn_x(x, 0)
            pe.wait_ge(key1_ready, 2)
            scores1(0)
            scores1(1)
            pe.wait_ge(x2_ready, 2)
            turn_x(x, 1)
            scores1(2)
            scores1(3)
            pe.wait_ge(val1_ready, B)
            for t in range(B * T):
                if t + 4 < B * T:
                    scores1(t + 4)
                if t == 7:
                    pe.wait_ge(xn_ready, B + 1)
                    turn_x(xn, 0)
                if t >= ATTEND_LATE:
                    turn1(t)
                if t >= 1:
                    attend1(t - 1)
                if t < ATTEND_LATE:
                    turn1(t)

            def three_passes(banks, wh, wl, xh, xl, start, stop):
                for n, (w, x) in enumerate(((wh, xh), (wh, xl), (wl, xh))):
                    for half, o in enumerate(banks):
                        last = mm(bank(o), w, x[:, S * half:S * half + S], start=start and n == 0, stop=stop and n == 2)
                return last

            def router(b):
                pe.wait_ge(xl_ready, b + 1)
                for t in range(T):
                    cols = slice(S * b + P * t, S * b + P * t + P)
                    o = bank(3)[:, E * (T * b + t):E * (T * b + t) + E]
                    mm(o, xh[:, cols], wgT[:, 0, :], stop=False)
                    mm(o, xh[:, cols], wgT[:, 1, :], start=False, stop=False)
                    last = mm(o, xl[:, cols], wgT[:, 0, :], start=False)
                last.then_inc(logit_psum, 1)

            def turn_combine():
                pe.wait_ge(combine_ready, 1)
                for b in range(B):
                    for t in range(T):
                        last = turn(bank(4 + b)[0:E, P * t:P * t + P], combine[:, T * b + t, :])
                    last.then_inc(combineT_psum, 1)

            def half_product1(u):
                half, k = u // PAIR, u % PAIR
                if k == 0:
                    pe.wait_ge(xl_ready, half + 1)
                if k % FC == 0:
                    pe.wait_ge(w1_split, k // FC + 1)
                if u == 0:
                    pe.wait_ge(p1T_ready, B * T - 1)
                if u == 1:
                    pe.wait_ge(added1, B * T - 1)
                if u >= 2:
                    pe.wait_ge(gelu_done, u - 1)
                cols = slice(S * half, S * half + S)
                three_passes((6 + u % 2,), w1h[:, k // FC, k % FC, :], w1l[:, k // FC, k % FC, :], xh[:, cols],
                             xl[:, cols], True, True).then_inc(mm1_done, 1)

            def half_product2(u):
                half, k = u // PAIR, u % PAIR
                if k % FC == 0:
                    pe.wait_ge(w2_split, k // FC + 1)
                pe.wait_ge(lo_done, u + 1)
                three_passes((2 * (k // FC) + half,), w2h[:, k // FC, k % FC, :], w2l[:, k // FC, k % FC, :],
                             hh_half[:, u % 8, :], hl_half[:, u % 8, :], k % FC == 0,
                             k % FC == FC - 1).then_inc(mm2_done, 1)

            for u in range(2 * PAIR):
                half_product1(u)
                if u == 0:
                    attend1(B * T - 1)
                if u == ROUTER0:
                    router(0)
                if u == TURN1:
                    pe.wait_ge(xn_ready, B + 2)
                    turn_x(xn, 1)
                if u == ROUTER1:
                    router(1)
                if u >= LAG:
                    half_product2(u - LAG)

            def product2(k, e, u):
                slot = k // FC
                if k % FC == 0:
                    pe.wait_ge(w2_split, e + 1)
                    pe.wait_ge(y_used, e * 2 - 2)
                pe.wait_ge(lo_done, u + 1)
                three_passes((2 * slot, 2 * slot + 1), w2h[:, slot, k % FC, :], w2l[:, slot, k % FC, :],
                             hh[:, k % 4, :], hl[:, k % 4, :], k % FC == 0, k % FC == FC - 1).then_inc(mm2_done, 1)

            def pair(it, first):
                for k in range(PAIR):
                    u, slot = it * PAIR + k, k // FC
                    if k % FC == 0:
                        pe.wait_ge(w1_split, it * 2 + (slot - 1))
                    if first and k == 0:
                        pe.wait_ge(gelu_done, u)
                    elif first and k == 1:
                        pe.wait_ge(combineT_ready, B)
                    else:
                        pe.wait_ge(gelu_done, u - 1)
                    three_passes((6 - 2 * (k % 2), 7 - 2 * (k % 2)), w1h[:, slot, k % FC, :], w1l[:, slot, k % FC, :],
                                 xh[:, :], xl[:, :], True, True).then_inc(mm1_done, 1)
                    if first and k == 0:
                        turn_combine()
                    if k >= LAG:
                        product2(k - LAG, it * 2 + ((k - LAG) // FC - 2), u - LAG)
                    elif first:
                        half_product2(u - LAG)
                    else:
                        product2(PAIR + k - LAG, None, u - LAG)

            pair(2, True)
            with pe.Fori(3, E // 2 + 1) as it:
                pair(it, False)
            product2(PAIR - 2, E - 1, E // 2 * PAIR + PAIR - 2)
            def turn_add(n, src, first):
                b, tiles, o = PIECES[n]
                for m, t in enumerate(range(tiles.start, tiles.stop)):
                    last = mm(bank(o)[:, D * m:D * m + D], src[:, S * b + P * t:S * b + P * t + P], ident,
                              start=first and m == 0, stop=not first)
                return last

            pe.wait_ge(y_used, B * (E - 1))
            for n in range(len(PIECES)):
                pe.wait_ge(sum_ready, B * (E - 2) + PIECES[n][0] + 1)
                turn_add(n, acc, True)
            k = PAIR - 1
            pe.wait_ge(lo_done, E // 2 * PAIR + k + 1)
            for half in range(2):
                cols = slice(S * half, S * half + S)
                three_passes((2 + half,), w2h[:, 1, k % FC, :], w2l[:, 1, k % FC, :], hh[:, k % 4, cols],
                             hl[:, k % 4, cols], False, True).then_inc(last_y, 1)
            for n in range(len(PIECES)):
                pe.wait_ge(y_used, B * (E - 1) + n + 1)
                turn_add(n, part.rearrange("d b n -> d (b n)"), False).then_inc(y_turned, 1)

        @block.vector
        def _(dve):
            v = nc.vector
            steps = [0]

            def done(ins):
                steps[0] += 1
                ins.then_inc(dve_step, 1)
                dve.wait_ge(dve_step, steps[0])

            def take_moments(b):
                for t in range(T):
                    last = v.bn_stats(stats[:, b, t, :], x[:, b, t, :])
                done(last)
                for t in range(T):
                    last = v.bn_aggr(moments[:, b, t, :], stats[:, b, t, :])
                last.then_inc(moments_ready, 1)

            def normalize(n, b):
                dve.wait_ge(rstd_ready, B * n + b + 1)
                for t in range(T):
                    last = v.tensor_scalar(xn[:, b, t, :], x[:, b, t, :], moments[:, b, t, 0:1], rstd[:, b, t:t + 1],
                                           ALU.subtract, ALU.mult)
                last.then_inc(xn_ready, 1)

            def wide(a, n):
                return a.unsqueeze(len(a.shape)).to_broadcast([*a.shape, n])

            def flat(a):
                return a.rearrange("p i d -> p (i d)")

            v.memset(zeros[:, :], 0.0).then_inc(zeros_ready, 1)
            v.memset(k1_band[:, :, :, :], 0.0)
            v.memset(v1_band, 0.0).then_inc(band_zero, 1)
            dve.wait_ge(setup0_in, 16)
            for b in range(B):
                last = v.tensor_copy(ctx_rep[:, b],
                                     ctxT[0:C + 1, J * b:J * b + J].unsqueeze(1).to_broadcast([C + 1, T, J]))
            last.then_inc(ctx_rep_ready, 1)
            dve.wait_ge(wq0T_psum, 1)
            v.tensor_copy(wq0T[:, :], bank(7)[:, 0:D])
            dve.wait_ge(kv0_psum, 1)
            v.tensor_copy(k0T[:, :, :].rearrange("d b j -> d (b j)"), bank(6)[:, 0:B * J]).then_inc(k0_ready, 1)
            dve.wait_ge(x_in[0], 16)
            take_moments(0)
            dve.wait_ge(kv0_psum, 2)
            dve.wait_ge(setup1_in, 16)
            for b in range(B):
                v.tensor_tensor(v0_band[:, b], bank(4)[:, P * b:P * b + P].unsqueeze(1).to_broadcast([P, T, D]),
                                wide(bandmask, D), ALU.mult).then_inc(v0_ready, 1)
            dve.wait_ge(key0_psum, 1)
            v.tensor_copy(key0[:, :, :].rearrange("d b j -> d (b j)"), bank(5)[:, 0:B * J])
            v.tensor_copy(bias0[:, :, :].rearrange("p b j -> p (b j)"),
                          bank(5)[:, B * J:2 * B * J]).then_inc(key0_ready, 1)
            dve.wait_ge(x_in[1], 16)
            take_moments(1)
            dve.wait_ge(key0_ready, 1)
            for b in range(B):
                s = bank(2 + b)[:, 0:P].rearrange("p (i j) -> p i j", j=J)
                dve.wait_ge(s0_psum, b + 1)
                dve.wait_ge(rstd_ready, b + 1)
                for t in range(T):
                    last = v.scalar_tensor_tensor(out=raw0[:, b, t, :], in0=s[:, t, :], scalar=rstd[:, b, t:t + 1],
                                                  in1=bias0[:, b, :], op0=ALU.mult, op1=ALU.add)
                done(last)
                done(v.tensor_reduce(small0[:, 0, b, :], raw0[:, b], X, ALU.max))
                v.tensor_tensor(shifted0[:, b], raw0[:, b], wide(small0[:, 0, b, :], J),
                                ALU.subtract).then_inc(sh0_ready, 1)
            for b in range(B):
                dve.wait_ge(e0_ready, b + 1)
                done(v.tensor_reduce(small0[:, 1, b, :], shifted0[:, b], X, ALU.add))
                done(v.reciprocal(small0[:, 2, b, :], small0[:, 1, b, :]))
                v.tensor_tensor(probs0[:, b], shifted0[:, b], wide(small0[:, 2, b, :], J), ALU.mult).then_inc(p0_ready, 1)
            dve.wait_ge(kv1_psum, 2)
            dve.wait_ge(band_zero, 1)
            for h in range(2):
                rows = slice(DH * h, DH * h + DH)
                last = v.tensor_scalar(k1_band[rows, :, h, :], bank(5)[rows, :].rearrange("p (c n) -> p c n", c=HC),
                                       DH ** -0.5, None, ALU.mult)
            last.then_inc(k1_ready, 1)
            dve.wait_ge(const_psum, 1)
            done(v.tensor_tensor(bias_t0[:, :], bank(1)[:, 0:3], bias_f[:, 0:3], ALU.add))
            v.tensor_scalar(bias_t0[:, 0:2], bias_t0[:, 0:2], 0.5, None, ALU.mult)
            v.tensor_scalar(bias_t1[:, 0:2], bias_f[:, 0:2], 0.5, None, ALU.mult)
            v.tensor_copy(bias_t1[:, 2:3], bias_f[:, 2:3]).then_inc(bias_ready, 1)


            def add0(b):
                dve.wait_ge(o0_psum, b + 1)
                v.tensor_tensor(flat(x[:, b]), bank(b), flat(x[:, b]), ALU.add).then_inc(added0, 1)

            add0(0)
            dve.wait_ge(added0, 1)
            take_moments(0)
            add0(1)
            normalize(1, 0)
            dve.wait_ge(added0, 2)
            take_moments(1)
            done(v.tensor_copy(wgT[:, 0, :], wgT_in))
            v.tensor_tensor(wgT[:, 1, :], wgT_in, wgT[:, 0, :].bitcast(F32), ALU.subtract)
            normalize(1, 1)
            dve.wait_ge(gates_ready, 1)
            v.tensor_scalar(keep_c, gates[:, 0, 0, :], 1.0, in_c, ALU.add, ALU.mult)
            dve.wait_ge(gates_ready, 3)
            done(v.scalar_tensor_tensor(out=new_c, in0=gates[:, 0, 1, :], scalar=1.0, in1=gates[:, 0, 2, :],
                                        op0=ALU.add, op1=ALU.mult))
            v.tensor_tensor(c1x2, keep_c, new_c, ALU.add).then_inc(c_ready, 1)
            dve.wait_ge(c_ready, 1)
            dve.wait_ge(gates_ready, 4)
            v.scalar_tensor_tensor(out=keep_c, in0=gates[:, 1, 0, :], scalar=1.0, in1=c1x2, op0=ALU.add, op1=ALU.mult)
            dve.wait_ge(gates_ready, 6)
            done(v.scalar_tensor_tensor(out=new_c, in0=gates[:, 1, 1, :], scalar=1.0, in1=gates[:, 1, 2, :],
                                        op0=ALU.add, op1=ALU.mult))
            v.scalar_tensor_tensor(out=c2x2, in0=keep_c, scalar=0.5, in1=new_c, op0=ALU.mult,
                                   op1=ALU.add).then_inc(c_ready, 1)
            for b in range(B):
                dve.wait_ge(h_psum, b + 1)
                v.tensor_tensor(flat(x[:, b]), bank(6 + b), flat(x[:, b]), ALU.add).then_inc(x2_ready, 1)
                dve.wait_ge(x2_ready, b + 1)
                take_moments(b)

            def max1(t):
                dve.wait_ge(s1_psum, t + 1)
                v.tensor_reduce(small1[:, 0, t % 3, :], bank(SCORE_BANKS[t % 4]).rearrange("p (h j) -> p h j", j=J), X,
                                ALU.max).then_inc(max1_done, 1)

            def shift1(t):
                dve.wait_ge(max1_done, t + 1)
                if t >= 3:
                    dve.wait_ge(p1_ready, t - 2)
                v.tensor_tensor(shifted1[:, t % 3], bank(SCORE_BANKS[t % 4]).rearrange("p (h j) -> p h j", j=J),
                                wide(small1[:, 0, t % 3, :], J), ALU.subtract).then_inc(sh1_ready, 1)

            def sum1(t):
                dve.wait_ge(e1_ready, t + 1)
                v.tensor_reduce(small1[:, 1, t % 3, :], shifted1[:, t % 3], X, ALU.add).then_inc(sum1_done, 1)

            def reciprocal1(t):
                dve.wait_ge(sum1_done, t + 1)
                v.reciprocal(small1[:, 2, t % 3, :], small1[:, 1, t % 3, :]).then_inc(r1_ready, 1)

            def add1(t):
                b, n = t // T, t % T
                dve.wait_ge(o1_step, t + 1)
                dve.wait_ge(x2b_ready, b + 1)
                v.tensor_tensor(x[:, b, n, :], bank((7, 1)[t % 2])[:, 0:D], x[:, b, n, :], ALU.add).then_inc(added1, 1)

            def stats1(t):
                dve.wait_ge(added1, t + 1)
                v.bn_stats(stats[:, t // T, t % T, :], x[:, t // T, t % T, :]).then_inc(stats1_ready, 1)

            def moments1(t):
                dve.wait_ge(stats1_ready, t + 1)
                last = v.bn_aggr(moments[:, t // T, t % T, :], stats[:, t // T, t % T, :])
                if t % T == T - 1:
                    last.then_inc(moments_ready, 1)

            def attended(t):
                add1(t)
                stats1(t)
                moments1(t)

            def x_lo(b):
                dve.wait_ge(xT_ready, 2 * B + b + 1)
                v.tensor_tensor(xl[:, S * b:S * b + S], bank(b), xh[:, S * b:S * b + S].bitcast(F32),
                                ALU.subtract).then_inc(xl_ready, 1)

            max1(0)
            shift1(0)
            max1(1)
            shift1(1)
            sum1(0)
            reciprocal1(0)
            max1(2)
            shift1(2)
            for t in range(1, B * T):
                if t + 2 < B * T:
                    max1(t + 2)
                if 3 <= t <= 5:
                    stats1(t - 3)
                sum1(t)
                if 3 <= t <= 5:
                    moments1(t - 3)
                if t + 2 < B * T:
                    shift1(t + 2)
                reciprocal1(t)
                if 2 <= t <= 4:
                    add1(t - 2)
                if t == 5:
                    attended(T - 1)
            normalize(3, 0)
            for t in range(T, B * T - 2):
                attended(t)
            x_lo(0)
            attended(B * T - 2)

            gs, gp, eq, first, rest, com = (a[:, :, :] for a in (g_shift, g_prob, g_eq, g_first, g_rest, combine))
            small = [g_small[:, n] for n in range(4)]
            down = descend.unsqueeze(1).to_broadcast([P, B * T, E])

            def router_shift(b):
                s = bank(3)[:, E * T * b:E * T * (b + 1)].rearrange("p (t e) -> p t e", e=E)
                top = g_small[:, 0, T * b:T * b + T]
                dve.wait_ge(logit_psum, b + 1)
                done(v.tensor_reduce(top, s, X, ALU.max))
                v.tensor_tensor(g_shift[:, T * b:T * b + T, :], s, wide(top, E), ALU.subtract).then_inc(gexp_arg, 1)

            def first_of(chosen):
                done(v.tensor_reduce(small[3], eq, X, ALU.max))
                done(v.tensor_tensor(chosen, eq, wide(small[3], E), ALU.is_equal))

            def pick_first():
                dve.wait_ge(gexp_arg, B)
                done(v.scalar_tensor_tensor(out=eq, in0=gs, scalar=0.0, in1=down, op0=ALU.is_equal, op1=ALU.mult))
                first_of(first)

            def pick_second():
                done(v.scalar_tensor_tensor(out=rest, in0=first, scalar=LOWEST, in1=gs, op0=ALU.mult, op1=ALU.add))
                done(v.tensor_reduce(small[2], rest, X, ALU.max))
                done(v.tensor_tensor(eq, rest, wide(small[2], E), ALU.is_equal))

            def both_picks():
                done(v.tensor_tensor(eq, eq, down, ALU.mult))
                first_of(com)
                done(v.tensor_tensor(eq, com, first, ALU.add))

            def router_weights():
                dve.wait_ge(gexp_ready, B)
                done(v.tensor_reduce(small[1], gp, X, ALU.add))
                done(v.reciprocal(small[2], small[1]))
                done(v.tensor_tensor(gp, gp, wide(small[2], E), ALU.mult))
                v.tensor_tensor(com, eq, gp, ALU.mult).then_inc(combine_ready, 1)

            def weigh(half, slot, e):
                cols = slice(S * half, S * half + S)
                static = isinstance(e, int)
                dve.wait_ge(mm2_done, e * FC + 3 * FC)
                for n in range(1, 2 if static and e == 1 else 3):
                    dve.wait_ge(cwb_in[n], 16)
                dve.wait_ge(sum_ready, e * 2 + (half - 1))
                w = cwb[:, e, cols] if static else cwb[:, bass.ds(e, 1), cols].rearrange("p e n -> p (e n)")
                v.scalar_tensor_tensor(out=part[:, half], in0=bank(2 * slot + half), scalar=b2T[:, bass.ds(e, 1)],
                                       in1=w, op0=ALU.add, op1=ALU.mult).then_inc(y_used, 1)
                dve.wait_ge(y_used, e * 2 + (half + 1))
                v.tensor_tensor(acc[:, cols], acc[:, cols], part[:, half], ALU.add).then_inc(sum_ready, 1)

            attended(B * T - 1)
            for u in range(2 * PAIR):
                dve.wait_ge(hi_done, u + 1)
                if u >= 8:
                    dve.wait_ge(mm2_done, u - 7)
                v.tensor_tensor(hl_half[:, u % 8, :], hid_half[:, u % 4, :], hh_half[:, u % 8, :].bitcast(F32),
                                ALU.subtract).then_inc(lo_done, 1)
                if u == 1:
                    normalize(3, 1)
                if u == X_LO1:
                    x_lo(1)
                if u == SHIFT0:
                    router_shift(0)
                if u == SHIFT1:
                    router_shift(1)
                if u == SHIFT1 + 1:
                    pick_first()
                if u == SHIFT1 + 2:
                    pick_second()
                if u == SHIFT1 + 3:
                    both_picks()
                if u == WEIGHTS:
                    router_weights()
                if u in (13, 14):
                    half = u - 13
                    dve.wait_ge(mm2_done, PAIR * half + FC)
                    v.tensor_copy(acc[:, S * half:S * half + S], bank(half)).then_inc(y_used, 1)
                if u == 15:
                    for b in range(B):
                        dve.wait_ge(combineT_psum, b + 1)
                        v.tensor_copy(combineT[:, S * b:S * b + S], bank(4 + b)[0:E, :]).then_inc(combineT_ready, 1)

            def pair(it, first):
                for k in range(PAIR):
                    u = it * PAIR + k
                    dve.wait_ge(hi_done, u + 1)
                    dve.wait_ge(mm2_done, u - 3)
                    v.tensor_tensor(hl[:, k % 4, :], hid[:, k % 2, :], hh[:, k % 4, :].bitcast(F32),
                                    ALU.subtract).then_inc(lo_done, 1)
                    if first and k == 2:
                        dve.wait_ge(cwb_in[0], 16)
                        dve.wait_ge(y_used, B)
                        for half in range(2):
                            cols = slice(S * half, S * half + S)
                            v.scalar_tensor_tensor(out=acc[:, cols], in0=acc[:, cols], scalar=b2T[:, 0:1],
                                                   in1=cwb[:, 0, cols], op0=ALU.add,
                                                   op1=ALU.mult).then_inc(sum_ready, 1)
                    if k in ((3, 4) if first else (1, 2)):
                        weigh((k + 1) % 2 if not first else k - 3, 1, it * 2 - 3)
                    if k in (5, 6):
                        weigh(k - 5, 0, it * 2 - 2)

            pair(2, True)
            with dve.Fori(3, E // 2 + 1) as it:
                pair(it, False)
            for b, tiles, _ in PIECES:
                dve.wait_ge(last_y, b + 1)
                dve.wait_ge(sum_ready, B * (E - 2) + b + 1)
                cols = slice(P * tiles.start, P * tiles.stop)
                v.scalar_tensor_tensor(out=part[:, b, cols], in0=bank(2 + b)[:, cols], scalar=b2T[:, E - 1:E],
                                       in1=cwb[:, E - 1, S * b + cols.start:S * b + cols.stop], op0=ALU.add,
                                       op1=ALU.mult).then_inc(y_used, 1)
            for n, (b, tiles, o) in enumerate(PIECES):
                dve.wait_ge(y_turned, n + 1)
                v.tensor_tensor(flat(x[:, b, tiles]), bank(o)[:, 0:D * T // 2], flat(x[:, b, tiles]),
                                ALU.add).then_inc(res_ready, 1)


NAMES = ["x", "xT", "setup0", "setup1", "gate_T", "wq1", "wk1", "wv1", "wo1", "bo1", "w1", "w2"]


def lay_out(a):
    import numpy as np

    def rows(parts, pack):
        out = np.zeros((P, sum(n for _, n in pack)), np.float32)
        at = 0
        for name, n in pack:
            p = parts[name]
            out[:p.shape[0], at:at + n] = p
            at += n
        return out

    one = np.ones((1, B * J), np.float32)
    ident = np.eye(P, dtype=np.float32)
    p = np.arange(P)[:, None]
    setup0 = {
        "ctxT": np.concatenate([a["ctx_768"].reshape(B * J, C).T, one]),
        "wq0": a["L0_xattn_Wq"],
        "wk0": np.concatenate([a["L0_xattn_Wk"], a["L0_xattn_bk"][None]]),
        "wv0": np.concatenate([a["L0_xattn_Wv"], a["L0_xattn_bv"][None]]),
        "centre": ident - np.float32(1 / D),
        "bq0": a["L0_xattn_bq"][:, None],
    }
    setup1 = {
        "ident": ident,
        "bandmask": (p // J == np.arange(T)).astype(np.float32),
        "descend": np.tile(np.arange(E, 0, -1, dtype=np.float32), (P, 1)),
        "minus_half": np.full((P, T), -0.5, np.float32),
        "euler": np.full((P, T * E), np.e, np.float32),
        "bias_f": np.stack([a["L0_ffn_" + n] for n in ("bf", "bi", "bc", "bo")], axis=1),
        "in_c": a["L0_ffn_in_c"][:, None],
        "wgT": a["L1_ffn_w_gate"].T,
        "b2T": a["L1_ffn_b2"].T,
        "b1": a["L1_ffn_b1"].reshape(E, FC, P).transpose(2, 0, 1).reshape(P, E * FC),
    }
    return {
        "x": a["x"],
        "xT": a["x"].reshape(B, P, T, D).transpose(3, 0, 2, 1).reshape(D, B, S),
        "setup0": rows(setup0, PACK0),
        "setup1": rows(setup1, PACK1),
        "gate_T": np.stack([a["L0_ffn_" + n].T for n in ("wf", "wi", "wc", "wo", "uf", "ui", "uc", "uo")], axis=1),
        "wq1": a["L1_xattn_w_q"].reshape(D, HC, P),
        "wk1": a["L1_xattn_w_k"].reshape(C, HC, P),
        "wv1": a["L1_xattn_w_v"].reshape(C, HC, P),
        "wo1": a["L1_xattn_w_o"].reshape(HC, P, D).transpose(1, 0, 2),
        "bo1": a["L1_xattn_b_o"],
        "w1": a["L1_ffn_W1"].reshape(E, D, FC, P).transpose(1, 0, 2, 3),
        "w2": a["L1_ffn_W2"].reshape(E, FC, P, D).transpose(2, 0, 1, 3),
    }


def kernel(**inputs):
    import numpy as np
    import concourse.bacc as bacc
    from concourse.bass_utils import run_bass_kernel_spmd

    laid = lay_out({n: np.asarray(x) for n, x in inputs.items()})
    nc = bacc.Bacc("TRN2", target_bir_lowering=False, num_devices=1)
    arrays, views = {}, {}
    for name in NAMES:
        a = np.ascontiguousarray(laid[name])
        arrays[f"in_{name}"] = a
        views[name] = nc.dram_tensor(f"in_{name}", a.shape, mybir.dt.from_np(a.dtype), kind="ExternalInput").ap()
    out = nc.dram_tensor("out_x", (B, S, D), F32, kind="ExternalOutput").ap()
    two_layers(nc, views, out)
    r = run_bass_kernel_spmd(nc, [arrays], core_ids=[0])
    return r.results[0]["out_x"]
```
